# Optimizing a Trainium2 kernel written in Bass

```python
import numpy as np
import jax
import jax.numpy as jnp

def _softmax(x, axis=-1):
    return jax.nn.softmax(x, axis=axis)

def _gelu(x):
    return jax.nn.gelu(x, approximate=True)

def _silu(x):
    return jax.nn.silu(x)

def _sigmoid(x):
    return jax.nn.sigmoid(x)

def _layernorm(x, axis=-1, eps=1e-05):
    m = jnp.mean(x, axis=axis, keepdims=True)
    v = jnp.var(x, axis=axis, keepdims=True)
    return (x - m) / jnp.sqrt(v + eps)

def _scatter_add(tgt, idx, src, axis=0):
    return tgt.at[idx].add(src)

def _segment_sum(src, seg, n):
    return jax.ops.segment_sum(src, seg, n)
kernel_name = 'mk_macaron_d1_jaxref_r8_9536fc'

def setup_inputs(seed: int=0):
    np.random.seed(seed)
    _w = jnp.asarray

    def _L0_attn_setup():
        import jax, jax.numpy as jnp
        import numpy as np
        B, T, D, S = (8, 512, 256, 128)

        def _layernorm(x, gamma, beta, eps=1e-05):
            mu = jnp.mean(x, axis=-1, keepdims=True)
            var = jnp.var(x, axis=-1, keepdims=True)
            return (x - mu) * jax.lax.rsqrt(var + eps) * gamma + beta
        key = jax.random.key(seed)
        ks = jax.random.split(key, 9)
        sd = 0.02
        return {'x': jax.random.normal(ks[0], (B, T, D), dtype=jnp.float32), 'gamma': jnp.ones((D,), dtype=jnp.float32), 'beta': jnp.zeros((D,), dtype=jnp.float32), 'W_in': jax.random.normal(ks[1], (D, 3 * S), dtype=jnp.float32) * sd, 'b_in': jnp.zeros((3 * S,), dtype=jnp.float32), 'W_out': jax.random.normal(ks[2], (S, D), dtype=jnp.float32) * sd, 'b_out': jnp.zeros((D,), dtype=jnp.float32), 'W_skip': jax.random.normal(ks[3], (D, D), dtype=jnp.float32) * sd, 'b_skip': jnp.zeros((D,), dtype=jnp.float32)}
    _L0_attn_in = _L0_attn_setup()

    def _L0_ffn_setup():
        import jax, jax.numpy as jnp
        import numpy as np
        import math
        N_EMBD = 256
        N_HEAD = 16
        HEAD_DIM = N_EMBD // N_HEAD
        B, T = (2, 256)
        key = jax.random.key(seed)
        k1, k2, k3 = jax.random.split(key, 3)
        x = jax.random.normal(k1, (B, T, N_EMBD), dtype=jnp.float32)
        W_gate = jax.random.normal(k2, (N_HEAD, N_EMBD), dtype=jnp.float32) * 0.02
        W_qkv = jax.random.normal(k3, (3 * N_EMBD, N_EMBD), dtype=jnp.float32) * 0.02
        return {'x': x, 'W_gate': W_gate, 'W_qkv': W_qkv}
    _L0_ffn_in = _L0_ffn_setup()
    _d = {'L0_attn_x': _L0_attn_in['x'], 'L0_attn_gamma': _L0_attn_in['gamma'], 'L0_attn_beta': _L0_attn_in['beta'], 'L0_attn_W_in': _L0_attn_in['W_in'], 'L0_attn_b_in': _L0_attn_in['b_in'], 'L0_attn_W_out': _L0_attn_in['W_out'], 'L0_attn_b_out': _L0_attn_in['b_out'], 'L0_attn_W_skip': _L0_attn_in['W_skip'], 'L0_attn_b_skip': _L0_attn_in['b_skip'], 'L0_ffn_W_gate': _L0_ffn_in['W_gate'], 'L0_ffn_W_qkv': _L0_ffn_in['W_qkv']}
    _x0 = _d['L0_attn_x']
    _d['L0_attn_x'] = jax.random.normal(jax.random.fold_in(jax.random.key(seed), 1), (1, 2048, 256), dtype=_x0.dtype)
    del _x0
    return _d

def reference(L0_attn_x, L0_attn_gamma, L0_attn_beta, L0_attn_W_in, L0_attn_b_in, L0_attn_W_out, L0_attn_b_out, L0_attn_W_skip, L0_attn_b_skip, L0_ffn_W_gate, L0_ffn_W_qkv):

    def _L0_attn_ref(x, gamma, beta, W_in, b_in, W_out, b_out, W_skip, b_skip):
        import jax, jax.numpy as jnp
        import numpy as np
        B, T, D, S = (8, 512, 256, 128)

        def _layernorm(x, gamma, beta, eps=1e-05):
            mu = jnp.mean(x, axis=-1, keepdims=True)
            var = jnp.var(x, axis=-1, keepdims=True)
            return (x - mu) * jax.lax.rsqrt(var + eps) * gamma + beta
        u = _layernorm(x, gamma, beta)
        gates = jnp.einsum('btd,de->bte', u, W_in) + b_in
        S_ = W_out.shape[0]
        delta, b_proj, c_proj = (gates[..., :S_], gates[..., S_:2 * S_], gates[..., 2 * S_:])
        alpha = jax.nn.sigmoid(delta)
        tc = jnp.tanh(c_proj)

        def step(h, inp):
            a_t, b_t, tc_t = inp
            h = (1.0 - a_t) * h + a_t * b_t
            return (h, h * tc_t)
        h0 = jnp.zeros((x.shape[0], S_), dtype=x.dtype)
        _, y = jax.lax.scan(step, h0, (alpha.transpose(1, 0, 2), b_proj.transpose(1, 0, 2), tc.transpose(1, 0, 2)))
        y = y.transpose(1, 0, 2)
        out = jnp.einsum('bts,sd->btd', y, W_out) + b_out
        out = out + jnp.einsum('btd,de->bte', x, W_skip) + b_skip
        return out

    def _L0_ffn_ref(x, W_gate, W_qkv):
        import jax, jax.numpy as jnp
        import numpy as np
        import math
        N_EMBD = 256
        N_HEAD = 16
        HEAD_DIM = N_EMBD // N_HEAD
        B, T = (2, 256)
        Bb, Tt, C = x.shape
        H, hd = (N_HEAD, HEAD_DIM)
        gating = jax.nn.softmax(x @ W_gate.T, axis=-1)
        idx = jnp.argmax(gating, axis=-1)
        indicator = jax.nn.one_hot(idx, H, dtype=gating.dtype)
        top1_val = jnp.max(gating, axis=-1, keepdims=True)
        gating_top1 = indicator * top1_val
        qkv = x @ W_qkv.T
        q, k, v = jnp.split(qkv, 3, axis=-1)
        k = k.reshape(Bb, Tt, H, hd)
        v = v.reshape(Bb, Tt, H, hd)
        k_shared = jnp.einsum('bth,bthd->btd', indicator, k)
        v_shared = jnp.einsum('bth,bthd->btd', gating_top1, v)
        q = q.reshape(Bb, Tt, H, hd).transpose(0, 2, 1, 3)
        att = jnp.einsum('bhqd,bkd->bhqk', q, k_shared) * (1.0 / math.sqrt(hd))
        causal = jnp.tril(jnp.ones((Tt, Tt), dtype=bool))
        att = jnp.where(causal[None, None, :, :], att, -jnp.inf)
        att = jax.nn.softmax(att, axis=-1)
        y = jnp.einsum('bhqk,bkd->bhqd', att, v_shared)
        y = y.transpose(0, 2, 1, 3).reshape(Bb, Tt, C)
        return y
    x = L0_attn_x
    x = x + 0.5 * _L0_ffn_ref(_layernorm(x, axis=-1), L0_ffn_W_gate, L0_ffn_W_qkv)
    x = x + _L0_attn_ref(_layernorm(x, axis=-1), L0_attn_gamma, L0_attn_beta, L0_attn_W_in, L0_attn_b_in, L0_attn_W_out, L0_attn_b_out, L0_attn_W_skip, L0_attn_b_skip)
    x = x + 0.5 * _L0_ffn_ref(_layernorm(x, axis=-1), L0_ffn_W_gate, L0_ffn_W_qkv)
    return x

_drawn_inputs = setup_inputs


def setup_inputs(seed=0):
    import zlib

    import numpy as np

    out = dict(_drawn_inputs(seed))
    spreads = {'L0_attn_gamma': (1.0, 0.6),
     'L0_attn_beta': (0.0, 0.8),
     'L0_attn_b_in': (0.0, 0.8),
     'L0_attn_b_out': (0.0, 0.1),
     'L0_attn_b_skip': (0.0, 0.1)}
    factors = {'L0_attn_W_in': 3.771,
     'L0_attn_W_out': 3.696,
     'L0_ffn_W_gate': 4.967,
     'L0_ffn_W_qkv': 4.142}
    for name, (base, spread) in spreads.items():
        noise = np.random.default_rng([zlib.crc32(name.encode()), seed]).standard_normal(out[name].shape)
        drawn = base * np.exp(spread * noise) if base else spread * noise
        out[name] = jnp.asarray(drawn.astype(out[name].dtype))
    for name, factor in factors.items():
        out[name] = (out[name] * factor).astype(out[name].dtype)
    return out
```

```python
import concourse.bass as bass
from concourse import mybir
from contextlib import ExitStack

T = 2048
D = 256
H = 16
HD = D // H
S = 128
P = 128
EPS = 1e-5
NT = T // P
QW = 512
NCH = T // QW
TC = QW // P
GH = 4
NG = H // GH
NU = NCH * NG
UW = GH * QW
DC = D // P
VW = 32
LAG = 2
SCALE = 1.0 / HD ** 0.5
NEG = -1e30

Q_PART = (0, 0, 0, 1, 1, 2)
K_PART = (0, 1, 2, 0, 1, 0)
KQ = HD * len(Q_PART)
KM = KQ + 2

def key_tiles(c):
    return TC * (c + 1)

def slots(c):
    return 2 * key_tiles(c)

def max_banks(c):
    return GH * TC * c + GH // 2 * 5

def before(of, c):
    return NG * sum(of(i) for i in range(c))

KT_ALL, SLOT_ALL, MB_ALL = (before(f, NCH) for f in (key_tiles, slots, max_banks))


def max_pieces(c):
    banks = []
    for hh in range(GH):
        for i in range(TC):
            for cc in range(c):
                banks.append([(hh, i, cc * QW, QW, 0, cc)])
    k0 = c * QW
    for hh in range(0, GH, 2):
        for h in (hh, hh + 1):
            banks.append([(h, 0, k0, P, 0, c), (h, 2, k0, 3 * P, P, c)])
            banks.append([(h, 3, k0, 4 * P, 0, c)])
        banks.append([(hh, 1, k0, 2 * P, 0, c), (hh + 1, 1, k0, 2 * P, 2 * P, c)])
    assert len(banks) == max_banks(c)
    return banks


def spread(steps, fills, tail):
    out, total, done, put = [], sum(s[2] for s in steps), 0, 0
    n = max(0, fills - tail)
    for s in steps:
        out.append(s)
        done += s[2]
        while put < n and put < n * done / total:
            out.append(("max", put, 0))
            put += 1
    while put < fills:
        out.append(("max", put, 0))
        put += 1
    return out


def unit_steps(c, mc, with_row):
    steps = []
    n = key_tiles(c)
    for j in range(n):
        w = QW - P * max(0, j - TC * c)
        steps.append(("qk", (j, 0), 2 * w))
        steps.append(("qk", (j, 1), 2 * w))
        if j:
            steps.append(("pv", j - 1, 4 * w))
        if j == 1 and with_row:
            steps.append(("row", None, 0))
    steps.append(("pv", n - 1, 4 * P))
    return spread(steps, 0 if mc is None else max_banks(mc), 3)


def macaron_block(nc, x, gamma, beta, w_in, b_in, w_out, b_out, w_skip, b_skip, w_gate, w_qkv, out):
    f32, bf16 = mybir.dt.float32, mybir.dt.bfloat16
    ALU, ACT, AX = mybir.AluOpType, mybir.ActivationFunctionType, mybir.AxisListType.X

    q_scratch = nc.dram_tensor("q_scratch", (2 * NCH, 3, DC, P, QW), bf16, kind="Internal").ap()

    ctx = ExitStack()
    with ctx:
        def sb(name, shape, dt=f32):
            return ctx.enter_context(nc.sbuf_tensor(name, shape, dt))

        def pb(name, shape, dt=f32):
            return ctx.enter_context(nc.psum_tensor(name, shape, dt))

        def sem(name):
            return ctx.enter_context(nc.semaphore(name))

        x_sb = sb("x_sb", [P, NT, D])
        wqkv_n = sb("wqkv_n", [P, 6, D])
        wg_n = sb("wg_n", [H, D])
        wqkv_t = sb("wqkv_t", [P, DC, 3 * D])
        wg_t = sb("wg_t", [P, DC, H])
        w_in_sb = sb("w_in_sb", [P, DC, 3 * S])
        w_skip_sb = sb("w_skip_sb", [P, DC, D])
        w_out_sb = sb("w_out_sb", [P, D])
        gamma_c = sb("gamma_c", [P, DC])
        beta_c = sb("beta_c", [P, DC])
        b_in_c = sb("b_in_c", [P, 3])
        b_out_r = sb("b_out_r", [P, D])
        b_skip_r = sb("b_skip_r", [P, D])
        b_sum = sb("b_sum", [P, D])
        ident = sb("ident", [P, P])
        ident_b = sb("ident_b", [P, P], bf16)
        mask_kq = sb("mask_kq", [P, P], bf16)
        mask_qk = sb("mask_qk", [P, P], bf16)
        rank = sb("rank", [P, TC, H])
        eps_c = sb("eps_c", [P, 1])
        stats = sb("stats", [P, TC, 6])
        mv = sb("mv", [P, TC, 2])
        std = sb("std", [P, TC])
        rstd = sb("rstd", [P, TC])
        u = sb("u", [P, TC, D])
        u2 = sb("u2", [P, TC, D])
        ut = sb("ut", [P, DC, QW])
        gmx = sb("gmx", [P, TC])
        gd = sb("gd", [P, TC, H])
        ge = sb("ge", [P, TC, H])
        gs = sb("gs", [P, TC])
        top = sb("top", [P, TC])
        cand = sb("cand", [P, TC, H])
        cmx = sb("cmx", [P, TC])
        pick = sb("pick", [P, TC, 2, H])
        prod = sb("prod", [P, 2 * D])
        kv = sb("kv", [P, TC, 2 * HD])
        k_rest = sb("k_rest", [P, TC, HD])
        k_rows = sb("k_rows", [P, TC, P], bf16)
        k_t = sb("k_t", [P, T], bf16)
        v_sb = sb("v_sb", [P, NT, VW])
        q_part = sb("q_part", [P, 3, DC, QW], bf16)
        q_rest = sb("q_rest", [P, DC, QW])
        q_t = sb("q_t", [P, NU * UW], bf16)
        mxp = sb("mxp", [P, GH * TC, NCH])
        mxf = sb("mxf", [P, GH * TC])
        mx2 = sb("mx2", [P, 2 * GH * TC], bf16)
        m_row = sb("m_row", [2 * GH * TC, P], bf16)
        probs = sb("probs", [P, 2, GH, QW])
        o_sb = sb("o_sb", [P, QW])
        rec = sb("rec", [P, GH * TC])
        y_att = sb("y_att", [P, GH * TC, HD])
        g_xt = sb("g_xt", [P, DC, QW])
        alpha = sb("alpha", [P, QW])
        keep = sb("keep", [P, QW])
        inp = sb("inp", [P, QW])
        tc_sb = sb("tc_sb", [P, QW])
        hst = sb("hst", [P, 2, QW])
        y_rec = sb("y_rec", [P, QW])

        ps_s = [pb(f"ps_s{i}", [P, 2, QW]) for i in range(2)]
        ps_x = [pb(f"ps_x{i}", [P, QW]) for i in range(2)]
        ps_o = pb("ps_o", [P, QW])
        ps_m = pb("ps_m", [P, QW])
        ps_ob = ps_o[:, 0:QW // 2].bitcast(bf16)
        ps_mrow = ps_m[0:2 * GH * TC, 0:P // 2].bitcast(bf16)

        s_xld = [sem(f"s_xld{c}") for c in range(NCH)]
        s_wld = [sem(f"s_wld{i}") for i in range(4)]
        s_const = sem("s_const")
        s_identb = sem("s_identb")
        s_wt = sem("s_wt")
        s_wte = sem("s_wte")
        s_bsum = sem("s_bsum")
        s_var = sem("s_var")
        s_std = sem("s_std")
        s_ln = sem("s_ln")
        s_tp = sem("s_tp")
        s_ta = sem("s_ta")
        s_tb = sem("s_tb")
        s_gl = sem("s_gl")
        s_gd = sem("s_gd")
        s_ge = sem("s_ge")
        s_kvp = sem("s_kvp")
        s_kvr = sem("s_kvr")
        s_kv = sem("s_kv")
        s_krow = sem("s_krow")
        s_ktp = sem("s_ktp")
        s_kt = sem("s_kt")
        s_qp = sem("s_qp")
        s_q1 = sem("s_q1")
        s_qr = sem("s_qr")
        s_q3 = sem("s_q3")
        s_qw = sem("s_qw")
        s_qt = [sem(f"s_qt{i}") for i in range(len(Q_PART))]
        s_exp = sem("s_exp")
        s_qk = sem("s_qk")
        s_pv = sem("s_pv")
        s_xmm = sem("s_xmm")
        s_xrd = sem("s_xrd")
        s_c1 = sem("s_c1")
        s_c2 = sem("s_c2")
        s_mx = sem("s_mx")
        s_mt = sem("s_mt")
        s_mr = sem("s_mr")
        s_md = sem("s_md")
        s_oe = sem("s_oe")
        s_ot = sem("s_ot")
        s_rc = sem("s_rc")
        s_ya = sem("s_ya")
        s_xa = sem("s_xa")
        s_gp = sem("s_gp")
        s_al = sem("s_al")
        s_tc = sem("s_tc")
        s_kp = sem("s_kp")
        s_in = sem("s_in")
        s_h = sem("s_h")
        s_yr = sem("s_yr")
        s_rp = sem("s_rp")
        s_xb = sem("s_xb")
        s_x2 = sem("s_x2")
        s_dch = sem("s_dch")
        s_pch = sem("s_pch")
        s_out = sem("s_out")

        block = ctx.enter_context(nc.Block())

        def gate_ln(c, second):
            return NCH + 2 * c + second

        def pre_ln(l, c):
            return c if l == 0 else 3 * NCH + c

        def bands(c):
            return x_sb[:, TC * c:TC * c + TC, :]

        @block.sync
        def _(sp):
            for c in range(NCH):
                sp.dma_start(bands(c), x[0, c * QW:(c + 1) * QW, :].rearrange("(t p) d -> p t d", p=P))\
                    .then_inc(s_xld[c], 16)
                if c == 0:
                    sp.dma_start(wqkv_n[:, :, :], w_qkv.rearrange("(r p) d -> p r d", p=P))\
                        .then_inc(s_wld[0], 16)
                    sp.dma_start(wg_n[:, :], w_gate).then_inc(s_wld[0], 16)
            sp.dma_start(w_in_sb[:, :, :], w_in.rearrange("(a p) e -> p a e", p=P)).then_inc(s_wld[1], 16)
            sp.dma_start(w_skip_sb[:, :, :], w_skip.rearrange("(a p) e -> p a e", p=P)).then_inc(s_wld[1], 16)
            sp.dma_start(w_out_sb[:, :], w_out).then_inc(s_wld[1], 16)
            sp.dma_start(gamma_c[:, :], gamma.rearrange("(a p) -> p a", p=P),
                         allow_slow_non_contiguous=True).then_inc(s_wld[2], 16)
            sp.dma_start(beta_c[:, :], beta.rearrange("(a p) -> p a", p=P),
                         allow_slow_non_contiguous=True).then_inc(s_wld[2], 16)
            sp.dma_start(b_in_c[:, :], b_in.rearrange("(a p) -> p a", p=P),
                         allow_slow_non_contiguous=True).then_inc(s_wld[2], 16)
            sp.dma_start(b_out_r[:, :], b_out.partition_broadcast(P)).then_inc(s_wld[3], 16)
            sp.dma_start(b_skip_r[:, :], b_skip.partition_broadcast(P)).then_inc(s_wld[3], 16)
            for l in range(2):
                for c in range(NCH):
                    n = NCH * l + c
                    sp.wait_ge(s_q1, 2 * n + 2)
                    sp.wait_ge(s_q3, 2 * n + 2)
                    sp.dma_start(q_scratch[n].rearrange("a b p t -> p a b t"), q_part[:, :, :, :])\
                        .then_inc(s_qw, 16)
                    sp.wait_ge(s_qw, 16 * (n + 1))
                    for r, part in enumerate(Q_PART):
                        for b in range(DC):
                            w = UW * NG // DC
                            o = c * UW * NG + b * w
                            sp.dma_start(
                                q_t[HD * r:HD * r + HD, o:o + w].rearrange("p (h t) -> p h t", t=QW),
                                q_scratch[n, part, b].rearrange("(h d) t -> d h t", d=HD),
                            ).then_inc(s_qt[r], 16)

                def rows_of_maxima(v):
                    nv = NU * l + v
                    sp.wait_ge(s_mr, nv + 1)
                    sp.dma_start(q_t[KQ:KM, bass.ds(v * UW, UW)], m_row[:, :]).then_inc(s_md, 16)

                rows_of_maxima(0)
                with sp.Fori(1, NU) as v:
                    rows_of_maxima(v)
                if l == 1:
                    for c in range(NCH):
                        sp.wait_ge(s_xa, 1 + NU + NG * (c + 1))
                        sp.dma_start(out[0, c * QW:(c + 1) * QW, :].rearrange("(t p) d -> p t d", p=P),
                                     bands(c)).then_inc(s_out, 16)
            sp.wait_ge(s_out, 16 * NCH)

        @block.gpsimd
        def _(pool):
            g = nc.gpsimd
            n_own = [0]

            def own(ins):
                n_own[0] += 1
                ins.then_inc(s_pch, 1)
                pool.wait_ge(s_pch, n_own[0])

            pool.sem_inc(s_xa, 1)
            pool.sem_inc(s_md, 16)
            own(g.memset(ident[:, :], 0.0))
            own(g.affine_select(out=ident[:, :], in_=ident[:, :], compare_op=ALU.not_equal, fill=1.0,
                                base=0, pattern=[[-1, P]], channel_multiplier=1))
            own(g.tensor_copy(ident_b[:, :], ident[:, :]))
            own(g.memset(mask_kq[:, :], 0.0))
            own(g.memset(mask_qk[:, :], 0.0))
            own(g.affine_select(out=mask_kq[:, :], in_=mask_kq[:, :], compare_op=ALU.is_ge, fill=NEG,
                                base=0, pattern=[[1, P]], channel_multiplier=-1))
            own(g.affine_select(out=mask_qk[:, :], in_=mask_qk[:, :], compare_op=ALU.is_ge, fill=NEG,
                                base=0, pattern=[[-1, P]], channel_multiplier=1))
            own(g.memset(eps_c[:, :], EPS))
            for h in range(H):
                own(g.memset(rank[:, :, h:h + 1], float(H - h)))
            own(g.memset(k_rows[:, :, :], 0.0))
            own(g.memset(k_rows[:, :, KQ:KM], -1.0))
            own(g.memset(v_sb[:, :, :], 0.0))
            g.memset(v_sb[:, :, HD:HD + 1], 2.0).then_inc(s_const, 1)
            pool.wait_ge(s_wld[3], 32)
            g.tensor_tensor(b_sum[:, :], b_out_r[:, :], b_skip_r[:, :], op=ALU.add).then_inc(s_bsum, 1)
            pool.wait_ge(s_const, 1)
            pool.wait_ge(s_bsum, 1)

            def pre(l, c):
                n = NCH * l + c
                for b in range(DC):
                    pool.wait_ge(s_qr, 2 * n + b + 1)
                    if b == 0 and n:
                        pool.wait_ge(s_qw, 16 * n)
                    own(g.tensor_copy(q_part[:, 1, b, :], q_rest[:, b, :]))
                    g.tensor_tensor(q_part[:, 2, b, :], q_rest[:, b, :], q_part[:, 1, b, :],
                                    op=ALU.subtract).then_inc(s_q3, 1)
                pool.wait_ge(s_kv, n + 1)
                if n:
                    pool.wait_ge(s_ktp, n)
                def part(i):
                    return k_rows[:, :, HD * i:HD * i + HD]
                own(g.tensor_copy(part(0), kv[:, :, 0:HD]))
                own(g.tensor_tensor(k_rest[:, :, :], kv[:, :, 0:HD], part(0), op=ALU.subtract))
                own(g.tensor_copy(part(1), k_rest[:, :, :]))
                own(g.tensor_tensor(part(2), k_rest[:, :, :], part(1), op=ALU.subtract))
                g.tensor_copy(part(3), part(0))
                g.tensor_copy(part(4), part(1))
                g.tensor_copy(part(5), part(0))
                g.tensor_copy(v_sb[:, TC * c:TC * c + TC, 0:HD], kv[:, :, HD:2 * HD]).then_inc(s_krow, 1)

            def add_unit(l, c, hf, it):
                un = NU * l + NG * c + 2 * hf + it
                pool.wait_ge(s_ya, un + 2)
                xs = x_sb[:, TC * c:TC * c + TC, bass.ds(it * GH * HD + 2 * hf * GH * HD, GH * HD)]
                g.tensor_tensor(xs, xs, y_att[:, :, :].rearrange("p (i h) d -> p i (h d)", h=GH),
                                op=ALU.add).then_inc(s_xa, 1)

            for l in range(2):
                for c in range(NCH):
                    pre(l, c)
                for c in range(NCH):
                    for hf in range(2):
                        with pool.Fori(0, 2) as it:
                            add_unit(l, c, hf, it)
                if l == 0:
                    for c in range(NCH):
                        pool.wait_ge(s_ln, gate_ln(c, 0) + 1)
                        g.tensor_tensor(bands(c), bands(c), b_sum[:, :].unsqueeze(1).to_broadcast([P, TC, D]),
                                        op=ALU.add).then_inc(s_xb, 1)
                        pool.wait_ge(s_al, c + 1)
                        if c:
                            pool.wait_ge(s_h, c)
                        g.tensor_scalar(keep[:, :], alpha[:, :], -1.0, 1.0, ALU.mult, ALU.add)\
                            .then_inc(s_kp, 1)
                        pool.wait_ge(s_h, c + 1)
                        pool.wait_ge(s_tc, c + 1)
                        if c:
                            pool.wait_ge(s_rp, 2 * c)
                        g.tensor_tensor(y_rec[:, :], hst[:, c % 2, :], tc_sb[:, :], op=ALU.mult)\
                            .then_inc(s_yr, 1)

        @block.scalar
        def _(act):
            a = nc.scalar
            act.sem_inc(s_exp, 2)
            act.sem_inc(s_oe, 1)

            def sqrt_of(k):
                act.wait_ge(s_var, k + 1)
                if k == 0:
                    act.wait_ge(s_const, 1)
                a.activation(std[:, :], mv[:, :, 1], ACT.Sqrt, bias=eps_c[:, 0:1]).then_inc(s_std, 1)

            for r in range(6):
                act.wait_ge(s_wt, r + 1)
                a.activation(wqkv_t[:, :, r * P:(r + 1) * P],
                             ps_s[r % 2][:, :, 0:P], ACT.Copy).then_inc(s_wte, 1)
            act.wait_ge(s_wt, 7)
            a.activation(wg_t[:, :, :], ps_x[0][:, 0:DC * H].rearrange("p (a h) -> p a h", a=DC), ACT.Copy)\
                .then_inc(s_wte, 1)

            def pre(l, c):
                n = NCH * l + c
                k = pre_ln(l, c)
                sqrt_of(k)
                act.wait_ge(s_tp, k + 1)
                if n:
                    act.wait_ge(s_qp, 2 * n)
                a.activation(ut[:, 0, :], ps_s[0][:, 0, :], ACT.Copy).then_inc(s_ta, 1)
                act.wait_ge(s_gd, n + 1)
                a.activation(ge[:, :, :], gd[:, :, :], ACT.Exp).then_inc(s_ge, 1)
                for b in range(DC):
                    act.wait_ge(s_qp, 2 * n + b + 1)
                    if b == 0 and n:
                        act.wait_ge(s_qw, 16 * n)
                    a.activation(q_part[:, 0, b, :], ps_s[1][:, b, :], ACT.Copy).then_inc(s_q1, 1)
                act.wait_ge(s_ktp, n + 1)
                a.activation(k_t[:, c * QW:(c + 1) * QW], ps_ob, ACT.Copy).then_inc(s_kt, 1)

            def row(l, v):
                nv = NU * l + v
                act.wait_ge(s_mt, nv + 2)
                act.wait_ge(s_md, 16 * nv + 16)
                a.activation(m_row[:, :], ps_mrow, ACT.Copy).then_inc(s_mr, 1)

            def unit(l, c, hf, it, with_row):
                un = NG * c + 2 * hf + it
                s0 = SLOT_ALL * l + before(slots, c) + 2 * hf * slots(c)
                k0 = KT_ALL * l + before(key_tiles, c) + 2 * hf * key_tiles(c)
                for j in range(key_tiles(c)):
                    i = max(0, j - TC * c)
                    for hp in range(2):
                        act.wait_ge(s_qk, it * slots(c) + (s0 + 2 * j + hp + 1))
                        if hp == 0:
                            act.wait_ge(s_pv, it * key_tiles(c) + (k0 + j + 1))
                        a.activation(probs[:, j % 2, 2 * hp:2 * hp + 2, P * i:QW],
                                     ps_s[hp][:, :, P * i:QW], ACT.Exp, scale=SCALE).then_inc(s_exp, 1)
                    if j == 2 and with_row:
                        row(l, un + 1)
                act.wait_ge(s_pv, it * key_tiles(c) + (k0 + key_tiles(c) + 2))
                a.activation(o_sb[:, :], ps_o[:, :], ACT.Copy).then_inc(s_oe, 1)

            def recurrence(c):
                k = gate_ln(c, 0)
                sqrt_of(k)
                act.wait_ge(s_tp, k + 1)
                if c:
                    act.wait_ge(s_rp, 2 * c)
                a.activation(g_xt[:, 0, :], ps_s[0][:, 0, :], ACT.Copy).then_inc(s_ta, 1)
                sqrt_of(k + 1)
                act.wait_ge(s_tp, k + 2)
                if c == 0:
                    act.wait_ge(s_wld[2], 48)
                a.activation(ut[:, 0, :], ps_s[1][:, 0, :], ACT.Identity, scale=gamma_c[:, 0:1],
                             bias=beta_c[:, 0:1]).then_inc(s_ta, 1)
                act.wait_ge(s_gp, 3 * c + 1)
                if c:
                    act.wait_ge(s_in, c)
                    act.wait_ge(s_kp, c)
                a.activation(alpha[:, :], ps_x[0][:, :], ACT.Sigmoid, bias=b_in_c[:, 0:1]).then_inc(s_al, 1)
                act.wait_ge(s_gp, 3 * c + 3)
                if c:
                    act.wait_ge(s_yr, c)
                a.activation(tc_sb[:, :], ps_m[:, :], ACT.Tanh, bias=b_in_c[:, 2:3]).then_inc(s_tc, 1)

            for l in range(2):
                for c in range(NCH):
                    pre(l, c)
                row(l, 0)
                for c in range(NCH):
                    for hf in range(2):
                        if c == NCH - 1 and hf == 1:
                            unit(l, c, hf, 0, True)
                            unit(l, c, hf, 1, False)
                        else:
                            with act.Fori(0, 2) as it:
                                unit(l, c, hf, it, True)
                if l == 0:
                    for c in range(NCH):
                        recurrence(c)

        @block.vector
        def _(dve):
            v_ = nc.vector
            dve.sem_inc(s_xrd, 2)
            dve.sem_inc(s_ya, 1)
            n_own = [0]

            def own(ins):
                n_own[0] += 1
                ins.then_inc(s_dch, 1)
                dve.wait_ge(s_dch, n_own[0])

            def layer_norm(k, src, dst):
                for t in range(TC):
                    last = v_.bn_stats(stats[:, t, :], src[:, t, :])
                own(last)
                for t in range(TC):
                    last = v_.bn_aggr(mv[:, t, :], stats[:, t, :])
                last.then_inc(s_var, 1)
                dve.wait_ge(s_std, k + 1)
                own(v_.reciprocal(rstd[:, :], std[:, :]))
                for t in range(TC):
                    last = v_.tensor_scalar(dst[:, t, :], src[:, t, :], mv[:, t, 0:1], rstd[:, t:t + 1],
                                            ALU.subtract, ALU.mult)
                last.then_inc(s_ln, 1)
                dve.wait_ge(s_ln, k + 1)

            def pre(l, c):
                n = NCH * l + c
                k = pre_ln(l, c)
                if l == 0:
                    dve.wait_ge(s_xld[c], 16)
                if k:
                    dve.wait_ge(s_tp, k)
                layer_norm(k, bands(c), u)
                dve.wait_ge(s_tp, k + 1)
                if n:
                    dve.wait_ge(s_qp, 2 * n)
                v_.tensor_copy(ut[:, 1, :], ps_s[0][:, 1, :]).then_inc(s_tb, 1)
                dve.wait_ge(s_gl, n + 1)
                gl = ps_m[:, 0:TC * H].rearrange("p (t h) -> p t h", t=TC)
                own(v_.tensor_reduce(gmx[:, :], gl, axis=AX, op=ALU.max))
                v_.tensor_tensor(gd[:, :, :], gl, gmx[:, :].unsqueeze(2).to_broadcast([P, TC, H]),
                                 op=ALU.subtract).then_inc(s_gd, 1)
                dve.wait_ge(s_gd, n + 1)
                own(v_.scalar_tensor_tensor(cand[:, :, :], gd[:, :, :], 0.0, rank[:, :, :],
                                            ALU.is_equal, ALU.mult))
                own(v_.tensor_reduce(cmx[:, :], cand[:, :, :], axis=AX, op=ALU.max))
                own(v_.tensor_tensor(pick[:, :, 0, :], cand[:, :, :],
                                     cmx[:, :].unsqueeze(2).to_broadcast([P, TC, H]), op=ALU.is_equal))
                dve.wait_ge(s_ge, n + 1)
                own(v_.tensor_reduce(gs[:, :], ge[:, :, :], axis=AX, op=ALU.add))
                own(v_.reciprocal(top[:, :], gs[:, :]))
                own(v_.tensor_tensor(pick[:, :, 1, :], pick[:, :, 0, :],
                                     top[:, :].unsqueeze(2).to_broadcast([P, TC, H]), op=ALU.mult))
                if n:
                    dve.wait_ge(s_krow, n)
                for t in range(TC):
                    m = TC * n + t
                    dve.wait_ge(s_kvp, m + 1)
                    w = pick[:, t, :, :].rearrange("p a h -> p (a h)")
                    v_.tensor_tensor(prod[:, :].rearrange("p (g d) -> p g d", d=HD),
                                     ps_x[t % 2][:, :].rearrange("p (g d) -> p g d", d=HD),
                                     w.unsqueeze(2).to_broadcast([P, 2 * H, HD]), op=ALU.mult)\
                        .then_inc(s_kvr, 1)
                    dve.wait_ge(s_kvr, m + 1)
                    last = v_.tensor_reduce(kv[:, t, :].rearrange("p (a d) -> p a d", a=2),
                                            prod[:, :].rearrange("p (a h d) -> p a d h", a=2, h=H),
                                            axis=AX, op=ALU.add)
                    if t < TC - 1:
                        own(last)
                    else:
                        last.then_inc(s_kv, 1)
                        dve.wait_ge(s_kv, n + 1)
                    if t % 2 == 0:
                        b = t // 2
                        dve.wait_ge(s_q1, 2 * n + b + 1)
                        if n:
                            dve.wait_ge(s_q3, 2 * n)
                        v_.tensor_tensor(q_rest[:, b, :], ps_s[1][:, b, :], q_part[:, 0, b, :],
                                         op=ALU.subtract).then_inc(s_qr, 1)

            def maxima(l, mc, mg0, it, todo):
                b0 = MB_ALL * l + before(max_banks, mc) + mg0 * max_banks(mc)
                for n, segs in todo:
                    dve.wait_ge(s_xmm, it * max_banks(mc) + (b0 + n + 1))
                    for hh, i, _, w, col, piece in segs:
                        last = v_.tensor_reduce(mxp[:, hh * TC + i, piece:piece + 1],
                                                ps_x[n % 2][:, col:col + w], axis=AX, op=ALU.max)
                    last.then_inc(s_xrd, 1)

            def join(l, mc, mg0, it):
                nv = NU * l + NG * mc + mg0
                b0 = MB_ALL * l + before(max_banks, mc) + mg0 * max_banks(mc)
                dve.wait_ge(s_xrd, it * max_banks(mc) + (b0 + max_banks(mc) + 2))
                v_.tensor_reduce(mxf[:, :], mxp[:, :, 0:mc + 1], axis=AX, op=ALU.max).then_inc(s_c1, 1)
                dve.wait_ge(s_c1, it + (nv + 1))
                dve.wait_ge(s_mt, it + (nv + 1))
                v_.tensor_copy(mx2[:, 0:GH * TC], mxf[:, :]).then_inc(s_c2, 1)
                dve.wait_ge(s_c2, it + (nv + 1))
                v_.tensor_tensor(mx2[:, GH * TC:], mxf[:, :], mx2[:, 0:GH * TC], op=ALU.subtract)\
                    .then_inc(s_mx, 1)
                dve.wait_ge(s_mx, it + (nv + 1))

            def unit(l, c, hf, it):
                un = NU * l + NG * c + 2 * hf
                mc, mg0 = (c, 2) if hf == 0 else (c + 1, 0)
                if mc < NCH:
                    maxima(l, mc, mg0, it, list(enumerate(max_pieces(mc))))
                    join(l, mc, mg0, it)
                dve.wait_ge(s_ot, it + (un + 1))
                o = ps_m[:, :].rearrange("p (g e) -> p g e", e=VW)
                v_.reciprocal(rec[:, :], o[:, :, HD]).then_inc(s_rc, 1)
                dve.wait_ge(s_rc, it + (un + 1))
                dve.wait_ge(s_xa, it + (un + 1))
                v_.tensor_tensor(y_att[:, :, :], o[:, :, 0:HD],
                                 rec[:, :].unsqueeze(2).to_broadcast([P, GH * TC, HD]), op=ALU.mult)\
                    .then_inc(s_ya, 1)
                dve.wait_ge(s_ya, it + (un + 2))

            def recurrence(c):
                k = gate_ln(c, 0)
                dve.wait_ge(s_xa, 1 + NG * (c + 1))
                dve.wait_ge(s_tp, k)
                layer_norm(k, bands(c), u)
                dve.wait_ge(s_tp, k + 1)
                if c:
                    dve.wait_ge(s_rp, 2 * c)
                v_.tensor_copy(g_xt[:, 1, :], ps_s[0][:, 1, :]).then_inc(s_tb, 1)
                layer_norm(k + 1, u, u2)
                dve.wait_ge(s_tp, k + 2)
                if c == 0:
                    dve.wait_ge(s_wld[2], 48)
                v_.tensor_scalar(ut[:, 1, :], ps_s[1][:, 1, :], gamma_c[:, 1:2], beta_c[:, 1:2],
                                 ALU.mult, ALU.add).then_inc(s_tb, 1)
                dve.wait_ge(s_al, c + 1)
                dve.wait_ge(s_gp, 3 * c + 2)
                v_.scalar_tensor_tensor(inp[:, :], ps_x[1][:, :], b_in_c[:, 1:2], alpha[:, :],
                                        ALU.add, ALU.mult).then_inc(s_in, 1)
                dve.wait_ge(s_in, c + 1)
                dve.wait_ge(s_kp, c + 1)
                h0 = hst[:, (c - 1) % 2, QW - 1:QW] if c else 0.0
                if c:
                    dve.wait_ge(s_yr, c)
                v_.tensor_tensor_scan(hst[:, c % 2, :], keep[:, :], inp[:, :], h0, ALU.mult, ALU.add)\
                    .then_inc(s_h, 1)
                dve.wait_ge(s_h, c + 1)
                dve.wait_ge(s_xb, c + 1)
                for i in range(2):
                    dve.wait_ge(s_rp, 2 * c + i + 1)
                    xs = x_sb[:, TC * c + 2 * i:TC * c + 2 * i + 2, :].rearrange("p t d -> p (t d)")
                    v_.tensor_tensor(xs, ps_s[0][:, i, :], xs, op=ALU.add).then_inc(s_x2, 1)

            for l in range(2):
                for c in range(NCH):
                    if l:
                        dve.wait_ge(s_x2, 2 * c + 2)
                    pre(l, c)
                for g0 in range(LAG):
                    maxima(l, 0, g0, 0, list(enumerate(max_pieces(0))))
                    join(l, 0, g0, 0)
                for c in range(NCH):
                    for hf in range(2):
                        if c == NCH - 1 and hf == 1:
                            unit(l, c, hf, 0)
                            unit(l, c, hf, 1)
                        else:
                            with dve.Fori(0, 2) as it:
                                unit(l, c, hf, it)
                if l == 0:
                    for c in range(NCH):
                        recurrence(c)

        @block.tensor
        def _(pe):
            mm, tr = nc.tensor.matmul, nc.tensor.transpose
            pe.sem_inc(s_pv, 2)
            pe.sem_inc(s_mt, 1)

            pe.wait_ge(s_const, 1)
            pe.wait_ge(s_wld[0], 32)
            for r in range(6):
                if r >= 2:
                    pe.wait_ge(s_wte, r - 1)
                for dc in range(DC):
                    last = tr(ps_s[r % 2][:, dc, 0:P], wqkv_n[:, r, dc * P:(dc + 1) * P], ident[:, :])
                last.then_inc(s_wt, 1)
            for dc in range(DC):
                last = tr(ps_x[0][:, dc * H:(dc + 1) * H], wg_n[:, dc * P:(dc + 1) * P], ident[0:H, 0:H])
            last.then_inc(s_wt, 1)
            pe.wait_ge(s_wte, 7)

            def transpose_rows(k, src, dst):
                pe.wait_ge(s_ln, k + 1)
                for dc in range(DC):
                    for t in range(TC):
                        last = tr(dst[:, dc, t * P:(t + 1) * P], src[:, t, dc * P:(dc + 1) * P], ident[:, :])
                last.then_inc(s_tp, 1)

            def pre(l, c):
                n = NCH * l + c
                k = pre_ln(l, c)
                if l and c == 0:
                    pe.wait_ge(s_x2, 2 * NCH)
                pe.wait_ge(s_ta, k)
                pe.wait_ge(s_tb, k)
                transpose_rows(k, u, ps_s[0])
                pe.wait_ge(s_ta, k + 1)
                pe.wait_ge(s_tb, k + 1)
                if n:
                    pe.wait_ge(s_gd, n)
                for t in range(TC):
                    for dc in range(DC):
                        last = mm(ps_m[:, t * H:(t + 1) * H], ut[:, dc, t * P:(t + 1) * P], wg_t[:, dc, :],
                                  start=dc == 0, stop=dc == DC - 1)
                last.then_inc(s_gl, 1)
                for t in range(TC):
                    m = TC * n + t
                    if m >= 2:
                        pe.wait_ge(s_kvr, m - 1)
                    for dc in range(DC):
                        last = mm(ps_x[t % 2][:, :], ut[:, dc, t * P:(t + 1) * P], wqkv_t[:, dc, D:3 * D],
                                  start=dc == 0, stop=dc == DC - 1)
                    last.then_inc(s_kvp, 1)
                    if t % 2 == 0:
                        b = t // 2
                        if n:
                            pe.wait_ge(s_qr, 2 * n)
                        for dc in range(DC):
                            last = mm(ps_s[1][:, b, :], wqkv_t[:, dc, b * P:(b + 1) * P], ut[:, dc, :],
                                      start=dc == 0, stop=dc == DC - 1)
                        last.then_inc(s_qp, 1)
                pe.wait_ge(s_krow, n + 1)
                if n:
                    pe.wait_ge(s_kt, n)
                for t in range(TC):
                    last = tr(ps_ob[:, t * P:(t + 1) * P], k_rows[:, t, :], ident_b[:, :])
                last.then_inc(s_ktp, 1)

            def max_bank(l, mc, mg0, it, n):
                b0 = MB_ALL * l + before(max_banks, mc) + mg0 * max_banks(mc)
                pe.wait_ge(s_xrd, it * max_banks(mc) + (b0 + n + 1))
                for hh, i, key, w, col, piece in max_pieces(mc)[n]:
                    diag = piece == mc
                    q0 = it * UW + ((NG * mc + mg0) * UW + hh * QW + i * P)
                    last = mm(ps_x[n % 2][:, col:col + w], q_t[0:KQ, bass.ds(q0, P)], k_t[0:KQ, key:key + w],
                              start=True, stop=not diag)
                    if diag:
                        last = mm(ps_x[n % 2][:, col + w - P:col + w], ident_b[:, :], mask_qk[:, :],
                                  start=False, stop=True)
                last.then_inc(s_xmm, 1)

            def unit(l, c, hf, it, with_row):
                u_loc = NG * c + 2 * hf
                un = NU * l + u_loc
                s0 = SLOT_ALL * l + before(slots, c) + 2 * hf * slots(c)
                k0 = KT_ALL * l + before(key_tiles, c) + 2 * hf * key_tiles(c)
                mc, mg0 = (c, 2) if hf == 0 else (c + 1, 0)
                pe.wait_ge(s_md, it * 16 + 16 * (un + 2))
                for kind, arg, _ in unit_steps(c, mc if mc < NCH else None, with_row):
                    if kind == "qk":
                        j, hp = arg
                        i = max(0, j - TC * c)
                        pe.wait_ge(s_exp, it * slots(c) + (s0 + 2 * j + hp + 1))
                        for hh in range(2):
                            q0 = it * UW + (u_loc * UW + (2 * hp + hh) * QW + P * i)
                            diag = j >= TC * c
                            last = mm(ps_s[hp][:, hh, P * i:QW], k_t[0:KM, j * P:(j + 1) * P],
                                      q_t[0:KM, bass.ds(q0, QW - P * i)], start=True, stop=not diag)
                            if diag:
                                last = mm(ps_s[hp][:, hh, P * i:P * i + P], ident_b[:, :], mask_kq[:, :],
                                          start=False, stop=True)
                        last.then_inc(s_qk, 1)
                    elif kind == "pv":
                        j = arg
                        i = max(0, j - TC * c)
                        pe.wait_ge(s_exp, it * slots(c) + (s0 + 2 * j + 4))
                        if j == 0:
                            pe.wait_ge(s_oe, it + (un + 1))
                        for hh in range(GH):
                            last = mm(ps_o[VW * hh:VW * hh + VW, P * i:QW], v_sb[:, j, :],
                                      probs[:, j % 2, hh, P * i:QW], start=j == 0, stop=j == key_tiles(c) - 1)
                        last.then_inc(s_pv, 1)
                    elif kind == "row":
                        nv = un + 1
                        pe.wait_ge(s_mx, it + (nv + 1))
                        pe.wait_ge(s_ya, it + (un + 1))
                        tr(ps_mrow, mx2[:, :], ident_b[:, :]).then_inc(s_mt, 1)
                    else:
                        max_bank(l, mc, mg0, it, arg)
                pe.wait_ge(s_oe, it + (un + 2))
                if with_row:
                    pe.wait_ge(s_mr, it + (un + 2))
                else:
                    pe.wait_ge(s_ya, it + (un + 1))
                for i in range(TC):
                    last = tr(ps_m[:, i * P:(i + 1) * P], o_sb[:, i * P:(i + 1) * P], ident[:, :])
                last.then_inc(s_ot, 1)

            def recurrence(c):
                k = gate_ln(c, 0)
                if c == 0:
                    pe.wait_ge(s_exp, SLOT_ALL + 2)
                    pe.wait_ge(s_ya, NU + 1)
                    pe.wait_ge(s_wld[1], 48)
                else:
                    pe.wait_ge(s_x2, 2 * c)
                transpose_rows(k, u, ps_s[0])
                transpose_rows(k + 1, u2, ps_s[1])
                pe.wait_ge(s_ta, k + 2)
                pe.wait_ge(s_tb, k + 2)
                for b, bank in enumerate((ps_x[0], ps_x[1], ps_m)):
                    if c:
                        pe.wait_ge((s_al, s_in, s_tc)[b], c)
                    for dc in range(DC):
                        last = mm(bank[:, :], w_in_sb[:, dc, b * S:(b + 1) * S], ut[:, dc, :],
                                  start=dc == 0, stop=dc == DC - 1)
                    last.then_inc(s_gp, 1)
                pe.wait_ge(s_yr, c + 1)
                for t in range(TC):
                    o = ps_s[0][:, t // 2, (t % 2) * D:(t % 2 + 1) * D]
                    mm(o, y_rec[:, t * P:(t + 1) * P], w_out_sb[:, :], start=True, stop=False)
                    mm(o, g_xt[:, 0, t * P:(t + 1) * P], w_skip_sb[:, 0, :], start=False, stop=False)
                    last = mm(o, g_xt[:, 1, t * P:(t + 1) * P], w_skip_sb[:, 1, :], start=False, stop=True)
                    if t % 2:
                        last.then_inc(s_rp, 1)

            for l in range(2):
                for c in range(NCH):
                    pre(l, c)
                pe.wait_ge(s_kt, NCH * (l + 1))
                for r in range(len(Q_PART)):
                    pe.wait_ge(s_qt[r], 16 * DC * NCH * (l + 1))
                pe.wait_ge(s_kvr, NT * (l + 1))
                pe.wait_ge(s_qr, 2 * NCH * (l + 1))
                for g0 in range(LAG):
                    for n in range(max_banks(0)):
                        max_bank(l, 0, g0, 0, n)
                    if g0 == 0:
                        pe.wait_ge(s_mx, NU * l + 1)
                        tr(ps_mrow, mx2[:, :], ident_b[:, :]).then_inc(s_mt, 1)
                for c in range(NCH):
                    for hf in range(2):
                        if c == NCH - 1 and hf == 1:
                            unit(l, c, hf, 0, True)
                            unit(l, c, hf, 1, False)
                        else:
                            with pe.Fori(0, 2) as it:
                                unit(l, c, hf, it, True)
                if l == 0:
                    for c in range(NCH):
                        recurrence(c)


_INS = ['L0_attn_x', 'L0_attn_gamma', 'L0_attn_beta', 'L0_attn_W_in', 'L0_attn_b_in', 'L0_attn_W_out',
        'L0_attn_b_out', 'L0_attn_W_skip', 'L0_attn_b_skip', 'L0_ffn_W_gate', 'L0_ffn_W_qkv']
_OUTS = [((1, T, D), 'float32')]


def kernel(**inputs):
    import numpy as _np
    import concourse.bacc as _bacc
    from concourse import mybir as _mybir
    from concourse.bass_utils import run_bass_kernel_spmd as _run

    nc = _bacc.Bacc("TRN2", target_bir_lowering=False, num_devices=1)
    arrays, args = {}, []
    for name in _INS:
        a = _np.ascontiguousarray(inputs[name])
        arrays[f"in_{name}_dram"] = a
        args.append(nc.dram_tensor(f"in_{name}_dram", a.shape, _mybir.dt.from_np(a.dtype), kind="ExternalInput").ap())
    for i, (shape, dtype) in enumerate(_OUTS):
        dt = _mybir.dt.from_np(_np.dtype(dtype))
        args.append(nc.dram_tensor(f"out_{i}_dram", shape, dt, kind="ExternalOutput").ap())
    macaron_block(nc, *args)
    r = _run(nc, [arrays], core_ids=[0])
    got = tuple(r.results[0][f"out_{i}_dram"] for i in range(len(_OUTS)))
    return got[0]
```

```python
import concourse.bass as bass
from concourse import mybir
from contextlib import ExitStack

T = 2048
D = 256
H = 16
HD = D // H
S = 128
P = 128
EPS = 1e-5
NT = T // P
QW = 512
NCH = T // QW
TC = QW // P
GH = 4
NG = H // GH
NU = NCH * NG
UW = GH * QW
DC = D // P
VW = 32
LAG = 2
RING = 3
HEAD = 2
TAIL = 3
WARM_UP = 5
SCALE = 1.0 / HD ** 0.5
NEG = -1e30

Q_PART = (0, 0, 1, 1, 2, 0)
K_PART = (0, 1, 0, 1, 0, 2)
KQ = HD * len(Q_PART)
KM = KQ + 2

def key_tiles(c):
    return TC * (c + 1)

def slots(c):
    return 2 * key_tiles(c)

def max_banks(c):
    return GH * TC * c + 1 + 2 * GH + GH // 2

def before(of, c):
    return NG * sum(of(i) for i in range(c))

KT_ALL, SLOT_ALL, MB_ALL = (before(f, NCH) for f in (key_tiles, slots, max_banks))


def max_pieces(c):
    banks = []
    for hh in range(GH):
        for i in range(TC):
            for cc in range(c):
                banks.append([(hh, i, cc * QW, QW, 0, cc)])
    k0 = c * QW
    banks.append([(hh, 0, k0, P, P * hh, c) for hh in range(GH)])
    for hh in range(GH):
        banks.append([(hh, 2, k0, 3 * P, 0, c)])
        banks.append([(hh, 3, k0, 4 * P, 0, c)])
        if hh % 2:
            banks.append([(h, 1, k0, 2 * P, 2 * P * (h % 2), c) for h in (hh - 1, hh)])
    assert len(banks) == max_banks(c)
    return banks


def spread(steps, fills, head, tail):
    out, total, done, put = [], sum(s[2] for s in steps), 0, 0
    n = max(0, fills - tail)
    while put < min(head, n):
        out.append(("max", put, 0))
        put += 1
    for s in steps:
        out.append(s)
        done += s[2]
        while put < n and put < n * done / total:
            out.append(("max", put, 0))
            put += 1
    while put < fills:
        out.append(("max", put, 0))
        put += 1
    return out


def unit_steps(c, mc, with_row):
    steps = []
    n = key_tiles(c)
    for j in range(n):
        w = QW - P * (j if j < TC else 0)
        steps.append(("qk", (j, 0), 2 * w))
        steps.append(("qk", (j, 1), 2 * w))
        if j:
            steps.append(("pv", j - 1, 4 * w))
        if j == 1 and with_row:
            steps.append(("row", None, 0))
    steps.append(("pv", n - 1, 4 * P))
    return spread(steps, 0 if mc is None else max_banks(mc), 0 if mc == c else HEAD, TAIL)


def ring(steps):
    return [a if kind == "max" else kind for kind, a, _ in steps if kind in ("max", "row")]


def key_tile(c, j):
    return (TC * c + j, j) if j < TC else (j - TC, 0)


def ahead(l, c, hf):
    if hf == 0:
        return l, c, LAG
    if c < NCH - 1:
        return l, c + 1, 0
    return (l + 1, 0, 0) if l == 0 else None


def pair_steps(l, c, hf, last):
    nxt = ahead(l, c, hf)
    return unit_steps(c, nxt and nxt[1], not last)


def pairs():
    return [(2 * NCH * l + 2 * c + hf, l, c, hf) for l in range(2) for c in range(NCH) for hf in range(2)]


def side_work():
    side = {b: [] for b in range(4 * NCH)}
    side[0] = [("norm", 0, 0), ("turn", 0, 0), ("norm", 0, 1), ("heads", 0, 0), ("turn", 0, 1),
               ("norm", 0, 2), ("keys", 0, 0), ("heads", 0, 1)]
    side[1] += [("keys", 0, 1), ("turn", 0, 2), ("norm", 0, 3), ("heads", 0, 2)]
    side[2] += [("keys", 0, 2)]
    side[3] += [("turn", 0, 3), ("norms", 0, 0), ("heads", 0, 3)]
    side[4] += [("keys", 0, 3)]
    for c in range(NCH):
        at = side[2 * c + 4]
        at += [("turns", 0, c)]
        if c:
            at += [("norm", 1, c - 1), ("gates", 0, c), ("turn", 1, c - 1)]
        else:
            at += [("gates", 0, c)]
        if c < NCH - 1:
            at += [("norms", 0, c + 1)]
        if c:
            at += [("heads", 1, c - 1)]
            side[2 * c + 5] += [("keys", 1, c - 1)]
        at += [("branch", 0, c)]
    last = NCH - 1
    side[2 * last + 4] += [("norm", 1, last)]
    side[2 * last + 6] += [("turn", 1, last), ("heads", 1, last)]
    side[2 * last + 7] += [("keys", 1, last)]
    return side


SIDE = side_work()
ORDER = [s for b in sorted(SIDE) for s in SIDE[b]]


def norm_number(l, c):
    n = 0
    for kind, ll, cc in ORDER:
        if kind == "norm":
            if (ll, cc) == (l, c):
                return n
            n += 1
        elif kind == "norms":
            n += 2
    raise ValueError(l, c)


def keys_before(kind, l, c):
    return sum(k == "keys" for k, _, _ in ORDER[:ORDER.index((kind, l, c))])


def chunks_done(kind, l, c, hf):
    return sum(k == kind for b in range(2 * NCH * l + 2 * c + hf + 1) for k, _, _ in SIDE[b])


def heads_before(l, c):
    return sum(k == "heads" for k, _, _ in ORDER[:ORDER.index(("keys", l, c))])


def branch_number(c):
    n = 0
    for kind, _, cc in ORDER:
        if kind == "norms":
            if cc == c:
                return n
            n += 2
        n += kind == "norm"
    raise ValueError(c)


def macaron_block(nc, x, gamma, beta, w_in, b_in, w_out, b_out, w_skip, b_skip, w_gate, w_qkv, out):
    f32, bf16 = mybir.dt.float32, mybir.dt.bfloat16
    ALU, ACT, AX = mybir.AluOpType, mybir.ActivationFunctionType, mybir.AxisListType.X

    q_scratch = nc.dram_tensor("q_scratch", (2 * NCH, 3, DC, P, QW), bf16, kind="Internal").ap()

    ctx = ExitStack()
    with ctx:
        def sb(name, shape, dt=f32):
            return ctx.enter_context(nc.sbuf_tensor(name, shape, dt))

        def pb(name, shape, dt=f32):
            return ctx.enter_context(nc.psum_tensor(name, shape, dt))

        def sem(name):
            return ctx.enter_context(nc.semaphore(name))

        x_sb = sb("x_sb", [P, NT, D])
        wqkv_n = sb("wqkv_n", [P, 6, D])
        wg_n = sb("wg_n", [H, D])
        wqkv_t = sb("wqkv_t", [P, DC, 3 * D])
        wg_t = sb("wg_t", [P, DC, H])
        w_in_sb = sb("w_in_sb", [P, DC, 3 * S])
        w_skip_sb = sb("w_skip_sb", [P, DC, D])
        w_out_sb = sb("w_out_sb", [P, D])
        gamma_c = sb("gamma_c", [P, DC])
        beta_c = sb("beta_c", [P, DC])
        b_in_c = sb("b_in_c", [P, 3])
        b_out_r = sb("b_out_r", [P, D])
        b_skip_r = sb("b_skip_r", [P, D])
        b_sum = sb("b_sum", [P, D])
        ident = sb("ident", [P, P])
        ident_b = sb("ident_b", [P, P], bf16)
        half = sb("half", [P, TC])
        pace = sb("pace", [P, 2 * TC])
        mask_qk = sb("mask_qk", [P, P], bf16)
        rank = sb("rank", [P, TC, H])
        stats = sb("stats", [P, TC, 6])
        mv = sb("mv", [P, TC, 2])
        var = sb("var", [P, TC])
        rstd = sb("rstd", [P, TC])
        u = sb("u", [P, TC, D])
        u1 = sb("u1", [P, TC, D])
        u2 = sb("u2", [P, TC, D])
        ut = sb("ut", [P, DC, QW])
        u2t = sb("u2t", [P, DC, QW])
        gmx = sb("gmx", [P, TC])
        gd = sb("gd", [P, TC, H])
        ge = sb("ge", [P, TC, H])
        gs = sb("gs", [P, TC])
        top = sb("top", [P, TC])
        cand = sb("cand", [P, TC, H])
        cmx = sb("cmx", [P, TC])
        pick = sb("pick", [P, TC, 2, H])
        prod = sb("prod", [P, 2 * D])
        kv = sb("kv", [P, TC, 2 * HD])
        k_rest = sb("k_rest", [P, TC, HD])
        k_rows = sb("k_rows", [P, TC, P], bf16)
        k_tl = sb("k_tl", [P, 2, T], bf16)
        v_l = sb("v_l", [P, 2, NT, VW])
        q_part = sb("q_part", [P, 3, DC, QW], bf16)
        q_rest = sb("q_rest", [P, DC, QW])
        q_t = sb("q_t", [P, NU * UW], bf16)
        mxp = sb("mxp", [P, GH * TC, NCH])
        mxf = sb("mxf", [P, GH * TC])
        mx2 = sb("mx2", [P, 2 * GH * TC], bf16)
        m_row = sb("m_row", [2 * GH * TC, P], bf16)
        probs = sb("probs", [P, 2, GH, QW])
        o_sb = sb("o_sb", [P, QW])
        rec = sb("rec", [P, GH * TC])
        y_att = sb("y_att", [P, GH * TC, HD])
        g_xt = sb("g_xt", [P, DC, QW])
        th = sb("th", [P, QW])
        b_half = sb("b_half", [P, 1])
        alpha = sb("alpha", [P, QW])
        keep = sb("keep", [P, QW])
        inp = sb("inp", [P, QW])
        tc_sb = sb("tc_sb", [P, QW])
        hst = sb("hst", [P, 2, QW])
        y_rec = sb("y_rec", [P, QW])

        ps_s = [pb(f"ps_s{i}", [P, 2, QW]) for i in range(2)]
        ps_x = [pb(f"ps_x{i}", [P, QW]) for i in range(RING)]
        ps_o = pb("ps_o", [P, QW])
        ps_k = ps_s[1][:, 0, 0:QW // 2].bitcast(bf16)
        gate_logits = ps_s[0][:, 0, 0:TC * H]

        def gate_bank(t):
            return gate_logits[:, t * H:(t + 1) * H]

        def as_rows(bank):
            return bank[0:2 * GH * TC, 0:P // 2].bitcast(bf16)

        s_xld = [sem(f"s_xld{c}") for c in range(NCH)]
        s_wld = [sem(f"s_wld{i}") for i in range(4)]
        s_const = sem("s_const")
        s_ident = sem("s_ident")
        s_wt = sem("s_wt")
        s_wte = sem("s_wte")
        s_bsum = sem("s_bsum")
        s_var = sem("s_var")
        s_std = sem("s_std")
        s_ln = sem("s_ln")
        s_tp = sem("s_tp")
        s_ta = sem("s_ta")
        s_tb = sem("s_tb")
        s_gl = sem("s_gl")
        s_gd = sem("s_gd")
        s_ge = sem("s_ge")
        s_kvp = sem("s_kvp")
        s_kvr = sem("s_kvr")
        s_kv = sem("s_kv")
        s_k1 = sem("s_k1")
        s_kr = sem("s_kr")
        s_k2 = sem("s_k2")
        s_krow = sem("s_krow")
        s_ktp = sem("s_ktp")
        s_kt = sem("s_kt")
        s_qp = sem("s_qp")
        s_q1 = sem("s_q1")
        s_qr = sem("s_qr")
        s_q2 = sem("s_q2")
        s_q3 = sem("s_q3")
        s_qw = sem("s_qw")
        s_qt = [sem(f"s_qt{i}") for i in range(len(Q_PART))]
        s_exp = sem("s_exp")
        s_msk = sem("s_msk")
        s_qk = sem("s_qk")
        s_pv = sem("s_pv")
        s_xmm = sem("s_xmm")
        s_xrd = sem("s_xrd")
        s_c1 = sem("s_c1")
        s_c2 = sem("s_c2")
        s_mx = sem("s_mx")
        s_mt = sem("s_mt")
        s_mr = sem("s_mr")
        s_md = sem("s_md")
        s_oe = sem("s_oe")
        s_ot = sem("s_ot")
        s_rc = sem("s_rc")
        s_ya = sem("s_ya")
        s_xa = sem("s_xa")
        s_gp = sem("s_gp")
        s_al = sem("s_al")
        s_tc = sem("s_tc")
        s_kp = sem("s_kp")
        s_in = sem("s_in")
        s_h = sem("s_h")
        s_yr = sem("s_yr")
        s_rp = sem("s_rp")
        s_xb = sem("s_xb")
        s_x2 = sem("s_x2")
        s_dch = sem("s_dch")
        s_pch = sem("s_pch")
        s_out = sem("s_out")

        block = ctx.enter_context(nc.Block())

        def bands(c):
            return x_sb[:, TC * c:TC * c + TC, :]

        @block.sync
        def _(sp):
            for c in range(NCH):
                sp.dma_start(bands(c), x[0, c * QW:(c + 1) * QW, :].rearrange("(t p) d -> p t d", p=P))\
                    .then_inc(s_xld[c], 16)
            sp.dma_start(w_in_sb[:, :, :], w_in.rearrange("(a p) e -> p a e", p=P)).then_inc(s_wld[1], 16)
            sp.dma_start(w_skip_sb[:, :, :], w_skip.rearrange("(a p) e -> p a e", p=P)).then_inc(s_wld[1], 16)
            sp.dma_start(w_out_sb[:, :], w_out).then_inc(s_wld[1], 16)
            sp.dma_start(gamma_c[:, :], gamma.rearrange("(a p) -> p a", p=P),
                         allow_slow_non_contiguous=True).then_inc(s_wld[2], 16)
            sp.dma_start(beta_c[:, :], beta.rearrange("(a p) -> p a", p=P),
                         allow_slow_non_contiguous=True).then_inc(s_wld[2], 16)
            sp.dma_start(b_in_c[:, :], b_in.rearrange("(a p) -> p a", p=P),
                         allow_slow_non_contiguous=True).then_inc(s_wld[2], 16)
            sp.dma_start(b_out_r[:, :], b_out.partition_broadcast(P)).then_inc(s_wld[3], 16)
            sp.dma_start(b_skip_r[:, :], b_skip.partition_broadcast(P)).then_inc(s_wld[3], 16)

            def heads(l, c):
                n = NCH * l + c
                sp.wait_ge(s_q3, 2 * n + 2)
                sp.dma_start(q_scratch[n].rearrange("a b p t -> p a b t"), q_part[:, :, :, :])\
                    .then_inc(s_qw, 16)
                sp.wait_ge(s_qw, 16 * (n + 1))
                for r, part in enumerate(Q_PART):
                    for b in range(DC):
                        w = UW * NG // DC
                        o = c * UW * NG + b * w
                        sp.dma_start(
                            q_t[HD * r:HD * r + HD, o:o + w].rearrange("p (h t) -> p h t", t=QW),
                            q_scratch[n, part, b].rearrange("(h d) t -> d h t", d=HD),
                        ).then_inc(s_qt[r], 16)

            def rows_of_maxima(l, v):
                sp.wait_ge(s_mr, v + (NU * l + 1))
                sp.dma_start(q_t[KQ:KM, bass.ds(v * UW, UW)], m_row[:, :]).then_inc(s_md, 16)

            for b, l, c, hf in pairs():
                for kind, ll, cc in SIDE[b]:
                    if kind == "heads":
                        heads(ll, cc)
                if b == 0:
                    rows_of_maxima(0, 0)
                v = NG * c + 2 * hf + 1
                rows_of_maxima(l, v)
                if v + 1 < NU:
                    rows_of_maxima(l, v + 1)
                elif l == 0:
                    rows_of_maxima(1, 0)
                if l == 1 and hf == 1:
                    sp.wait_ge(s_xa, 1 + NU + NG * (c + 1))
                    sp.dma_start(out[0, c * QW:(c + 1) * QW, :].rearrange("(t p) d -> p t d", p=P),
                                 bands(c)).then_inc(s_out, 16)
            sp.wait_ge(s_out, 16 * NCH)

        @block.gpsimd
        def _(pool):
            g = nc.gpsimd
            n_own = [0]

            def own(ins):
                n_own[0] += 1
                ins.then_inc(s_pch, 1)
                pool.wait_ge(s_pch, n_own[0])

            pool.sem_inc(s_xa, 1)
            pool.sem_inc(s_md, 16)
            own(g.memset(ident[:, :], 0.0))
            g.affine_select(out=ident[:, :], in_=ident[:, :], compare_op=ALU.not_equal, fill=1.0,
                            base=0, pattern=[[-1, P]], channel_multiplier=1).then_inc(s_ident, 1)
            own(g.memset(half[:, :], -0.5))

            def constants():
                pool.wait_ge(s_ident, 1)
                for h in range(H):
                    g.memset(rank[:, :, h:h + 1], float(H - h))
                g.tensor_copy(ident_b[:, :], ident[:, :])
                g.memset(k_rows[:, :, 0:KQ], 0.0)
                g.memset(k_rows[:, :, KM:P], 0.0)
                g.memset(k_rows[:, :, KQ:KM], -1.0)
                own(g.memset(mask_qk[:, :], 0.0))
                g.affine_select(out=mask_qk[:, :], in_=mask_qk[:, :], compare_op=ALU.is_ge, fill=NEG,
                                base=0, pattern=[[-1, P]], channel_multiplier=1)
                g.memset(v_l[:, :, :, HD:HD + 1], 2.0)
                g.memset(v_l[:, :, :, HD + 1:VW], 0.0).then_inc(s_const, 1)
                pool.wait_ge(s_wld[2], 48)
                g.tensor_scalar(b_half[:, :], b_in_c[:, 0:1], 0.5, None, ALU.mult)
                pool.wait_ge(s_wld[3], 32)
                g.tensor_tensor(b_sum[:, :], b_out_r[:, :], b_skip_r[:, :], op=ALU.add).then_inc(s_bsum, 1)
                pool.wait_ge(s_const, 1)
                pool.wait_ge(s_bsum, 1)

            def rstd_of(k):
                pool.wait_ge(s_var, k + 1)
                own(g.tensor_scalar(var[:, :], mv[:, :, 1], EPS, None, ALU.add))
                g.tensor_tensor(rstd[:, :], var[:, :], half[:, :], op=ALU.pow).then_inc(s_std, 1)

            def heads(l, c):
                n = NCH * l + c
                for b in range(DC):
                    pool.wait_ge(s_q2, 2 * n + b + 1)
                    g.tensor_tensor(q_part[:, 2, b, :], q_rest[:, b, :], q_part[:, 1, b, :],
                                    op=ALU.subtract).then_inc(s_q3, 1)
                pool.wait_ge(s_k1, n + 1)
                g.tensor_tensor(k_rest[:, :, :], kv[:, :, 0:HD], k_rows[:, :, 0:HD], op=ALU.subtract)\
                    .then_inc(s_kr, 1)
                pool.wait_ge(s_kr, n + 1)
                pool.wait_ge(s_k2, n + 1)
                g.tensor_tensor(k_rows[:, :, KQ - HD:KQ], k_rest[:, :, :], k_rows[:, :, HD:2 * HD],
                                op=ALU.subtract).then_inc(s_krow, 1)

            def unit(l, c, hf, it):
                un = NU * l + NG * c + 2 * hf + it
                s0 = SLOT_ALL * l + before(slots, c) + 2 * hf * slots(c)
                for j in range(TC):
                    for hp in range(2):
                        pool.wait_ge(s_exp, it * slots(c) + (s0 + 2 * j + hp + 3))
                        g.tensor_tensor(pace[:, 2 * j + hp:2 * j + hp + 1], half[:, 0:1], half[:, 0:1],
                                        op=ALU.add)
                        pr = probs[:, j % 2, 2 * hp:2 * hp + 2, P * j:P * j + P]
                        g.affine_select(out=pr, in_=pr, compare_op=ALU.is_ge, fill=0.0, base=0,
                                        pattern=[[0, 2], [1, P]], channel_multiplier=-1).then_inc(s_msk, 1)
                pool.wait_ge(s_ya, un + 2)
                xs = x_sb[:, TC * c:TC * c + TC, bass.ds(it * GH * HD + 2 * hf * GH * HD, GH * HD)]
                g.tensor_tensor(xs, xs, y_att[:, :, :].rearrange("p (i h) d -> p i (h d)", h=GH),
                                op=ALU.add).then_inc(s_xa, 1)

            def norm(l, c):
                rstd_of(norm_number(l, c))

            def norms(l, c):
                k = branch_number(c)
                rstd_of(k)
                rstd_of(k + 1)

            def turns(l, c):
                pool.wait_ge(s_ln, branch_number(c) + 1)
                g.tensor_tensor(bands(c), bands(c), b_sum[:, :].unsqueeze(1).to_broadcast([P, TC, D]),
                                op=ALU.add).then_inc(s_xb, 1)

            def gates(l, c):
                pool.wait_ge(s_al, c + 1)
                if c:
                    pool.wait_ge(s_h, c)
                g.tensor_scalar(keep[:, :], th[:, :], -0.5, 0.5, ALU.mult, ALU.add)
                g.tensor_scalar(alpha[:, :], th[:, :], 0.5, 0.5, ALU.mult, ALU.add).then_inc(s_kp, 1)
                pool.wait_ge(s_h, c + 1)
                pool.wait_ge(s_tc, c + 1)
                if c:
                    pool.wait_ge(s_rp, 2 * c)
                g.tensor_tensor(y_rec[:, :], hst[:, c % 2, :], tc_sb[:, :], op=ALU.mult).then_inc(s_yr, 1)

            work = {"norm": norm, "norms": norms, "turns": turns, "heads": heads, "gates": gates}
            for b, l, c, hf in pairs():
                for kind, ll, cc in SIDE[b]:
                    if kind in work:
                        work[kind](ll, cc)
                        if (kind, ll, cc) == ORDER[0]:
                            constants()
                with pool.Fori(0, 2) as it:
                    unit(l, c, hf, it)

        @block.scalar
        def _(act):
            a = nc.scalar
            act.sem_inc(s_exp, 2)
            act.sem_inc(s_oe, 1)

            act.dma_start(wqkv_n[:, :, :], w_qkv.rearrange("(r p) d -> p r d", p=P)).then_inc(s_wld[0], 16)
            act.dma_start(wg_n[:, :], w_gate).then_inc(s_wld[0], 16)

            for r in range(6):
                act.wait_ge(s_wt, r + 1)
                a.activation(wqkv_t[:, :, r * P:(r + 1) * P],
                             ps_s[r % 2][:, :, 0:P], ACT.Copy).then_inc(s_wte, 1)
            act.wait_ge(s_wt, 7)
            a.activation(wg_t[:, :, :], ps_x[0][:, 0:DC * H].rearrange("p (a h) -> p a h", a=DC), ACT.Copy)\
                .then_inc(s_wte, 1)

            def turn(l, c):
                k = norm_number(l, c)
                n = NCH * l + c
                act.wait_ge(s_tp, k + 1)
                if n:
                    act.wait_ge(s_qp, 2 * n)
                a.activation(ut[:, 0, :], ps_s[0][:, 0, :], ACT.Copy).then_inc(s_ta, 1)

            def heads(l, c):
                n = NCH * l + c
                act.wait_ge(s_gd, n + 1)
                a.activation(ge[:, :, :], gd[:, :, :], ACT.Exp).then_inc(s_ge, 1)
                for b in range(DC):
                    act.wait_ge(s_qp, 2 * n + b + 1)
                    if b == 0 and n:
                        act.wait_ge(s_qw, 16 * n)
                    a.activation(q_part[:, 0, b, :], ps_s[1][:, b, :], ACT.Copy).then_inc(s_q1, 1)
                    act.wait_ge(s_qr, 2 * n + b + 1)
                    a.activation(q_part[:, 1, b, :], q_rest[:, b, :], ACT.Copy).then_inc(s_q2, 1)
                act.wait_ge(s_kv, n + 1)
                if n:
                    act.wait_ge(s_ktp, n)
                a.activation(v_l[:, l, TC * c:TC * c + TC, 0:HD], kv[:, :, HD:2 * HD], ACT.Copy)
                rows = k_rows[:, :, 0:KQ].rearrange("p t (g a d) -> p t g a d", g=3, a=2)
                a.activation(rows[:, :, :, 0, :], kv[:, :, 0:HD].unsqueeze(2).to_broadcast([P, TC, 3, HD]),
                             ACT.Copy).then_inc(s_k1, 1)
                act.wait_ge(s_kr, n + 1)
                a.activation(rows[:, :, 0:2, 1, :], k_rest[:, :, :].unsqueeze(2).to_broadcast([P, TC, 2, HD]),
                             ACT.Copy).then_inc(s_k2, 1)

            def keys(l, c):
                act.wait_ge(s_ktp, NCH * l + c + 1)
                a.activation(k_tl[:, l, c * QW:(c + 1) * QW], ps_k, ACT.Copy).then_inc(s_kt, 1)

            def row(l, v, bank):
                act.wait_ge(s_mt, v + (NU * l + 2))
                act.wait_ge(s_md, 16 * v + (16 * NU * l + 16))
                a.activation(m_row[:, :], as_rows(bank), ACT.Copy).then_inc(s_mr, 1)

            def unit(l, c, hf, it, with_row):
                s0 = SLOT_ALL * l + before(slots, c) + 2 * hf * slots(c)
                k0 = KT_ALL * l + before(key_tiles, c) + 2 * hf * key_tiles(c)
                uses = ring(pair_steps(l, c, hf, not with_row))
                for j in range(key_tiles(c)):
                    i = key_tile(c, j)[1]
                    for hp in range(2):
                        act.wait_ge(s_qk, it * slots(c) + (s0 + 2 * j + hp + 1))
                        if hp == 0:
                            act.wait_ge(s_pv, it * key_tiles(c) + (k0 + j + 1))
                        a.activation(probs[:, j % 2, 2 * hp:2 * hp + 2, P * i:QW],
                                     ps_s[hp][:, :, P * i:QW], ACT.Exp, scale=SCALE).then_inc(s_exp, 1)
                    if j == 2 and with_row:
                        row(l, it + (NG * c + 2 * hf + 1), ps_x[uses.index("row") % RING])
                act.wait_ge(s_pv, it * key_tiles(c) + (k0 + key_tiles(c) + 2))
                a.activation(o_sb[:, :], ps_o[:, :], ACT.Copy).then_inc(s_oe, 1)

            def turns(l, c):
                k = branch_number(c)
                act.wait_ge(s_tp, k + 1)
                if c == 0:
                    act.wait_ge(s_wld[2], 48)
                else:
                    act.wait_ge(s_gp, 3 * c)
                a.activation(u2t[:, 0, :], ps_s[1][:, 0, :], ACT.Identity, scale=gamma_c[:, 0:1],
                             bias=beta_c[:, 0:1]).then_inc(s_ta, 1)
                act.wait_ge(s_tp, k + 2)
                if c:
                    act.wait_ge(s_rp, 2 * c)
                a.activation(g_xt[:, 0, :], ps_s[0][:, 0, :], ACT.Copy).then_inc(s_ta, 1)

            def gates(l, c):
                act.wait_ge(s_gp, 3 * c + 1)
                if c:
                    act.wait_ge(s_kp, c)
                else:
                    act.wait_ge(s_bsum, 1)
                a.activation(th[:, :], ps_x[0][:, :], ACT.Tanh, bias=b_half[:, 0:1], scale=0.5)\
                    .then_inc(s_al, 1)
                act.wait_ge(s_gp, 3 * c + 3)
                if c:
                    act.wait_ge(s_yr, c)
                a.activation(tc_sb[:, :], ps_x[2][:, :], ACT.Tanh, bias=b_in_c[:, 2:3]).then_inc(s_tc, 1)

            work = {"turn": turn, "heads": heads, "keys": keys, "turns": turns, "gates": gates}
            for b, l, c, hf in pairs():
                for kind, ll, cc in SIDE[b]:
                    if kind in work:
                        work[kind](ll, cc)
                if b == 0:
                    row(0, 0, ps_o)
                if ahead(l, c, hf):
                    with act.Fori(0, 2) as it:
                        unit(l, c, hf, it, True)
                else:
                    unit(l, c, hf, 0, True)
                    unit(l, c, hf, 1, False)

        @block.vector
        def _(dve):
            v_ = nc.vector
            dve.sem_inc(s_xrd, 2)
            dve.sem_inc(s_ya, 1)
            n_own = [0]

            def own(ins):
                n_own[0] += 1
                ins.then_inc(s_dch, 1)
                dve.wait_ge(s_dch, n_own[0])

            def layer_norm(k, src, dst):
                for t in range(TC):
                    last = v_.bn_stats(stats[:, t, :], src[:, t, :])
                own(last)
                for t in range(TC):
                    last = v_.bn_aggr(mv[:, t, :], stats[:, t, :])
                last.then_inc(s_var, 1)
                dve.wait_ge(s_std, k + 1)
                for t in range(TC):
                    last = v_.tensor_scalar(dst[:, t, :], src[:, t, :], mv[:, t, 0:1], rstd[:, t:t + 1],
                                            ALU.subtract, ALU.mult)
                last.then_inc(s_ln, 1)
                dve.wait_ge(s_ln, k + 1)

            def norm(l, c):
                n = NCH * l + c
                if l == 0:
                    dve.wait_ge(s_xld[c], 16)
                else:
                    dve.wait_ge(s_x2, 2 * c + 2)
                if n:
                    dve.wait_ge(s_tp, norm_number(*divmod(n - 1, NCH)) + 1)
                layer_norm(norm_number(l, c), bands(c), u)

            def turn(l, c):
                n = NCH * l + c
                dve.wait_ge(s_tp, norm_number(l, c) + 1)
                if n:
                    dve.wait_ge(s_qp, 2 * n)
                v_.tensor_copy(ut[:, 1, :], ps_s[0][:, 1, :]).then_inc(s_tb, 1)

            def heads(l, c):
                n = NCH * l + c
                dve.wait_ge(s_gl, n + 1)
                gl = gate_logits.rearrange("p (t h) -> p t h", t=TC)
                own(v_.tensor_reduce(gmx[:, :], gl, axis=AX, op=ALU.max))
                v_.tensor_tensor(gd[:, :, :], gl, gmx[:, :].unsqueeze(2).to_broadcast([P, TC, H]),
                                 op=ALU.subtract).then_inc(s_gd, 1)
                dve.wait_ge(s_gd, n + 1)
                own(v_.scalar_tensor_tensor(cand[:, :, :], gd[:, :, :], 0.0, rank[:, :, :],
                                            ALU.is_equal, ALU.mult))
                own(v_.tensor_reduce(cmx[:, :], cand[:, :, :], axis=AX, op=ALU.max))
                own(v_.tensor_tensor(pick[:, :, 0, :], cand[:, :, :],
                                     cmx[:, :].unsqueeze(2).to_broadcast([P, TC, H]), op=ALU.is_equal))
                dve.wait_ge(s_ge, n + 1)
                own(v_.tensor_reduce(gs[:, :], ge[:, :, :], axis=AX, op=ALU.add))
                own(v_.reciprocal(top[:, :], gs[:, :]))
                own(v_.tensor_tensor(pick[:, :, 1, :], pick[:, :, 0, :],
                                     top[:, :].unsqueeze(2).to_broadcast([P, TC, H]), op=ALU.mult))
                if n:
                    dve.wait_ge(s_krow, n)
                for t in range(TC):
                    m = TC * n + t
                    dve.wait_ge(s_kvp, m + 1)
                    w = pick[:, t, :, :].rearrange("p a h -> p (a h)")
                    v_.tensor_tensor(prod[:, :].rearrange("p (g d) -> p g d", d=HD),
                                     ps_x[m % RING][:, :].rearrange("p (g d) -> p g d", d=HD),
                                     w.unsqueeze(2).to_broadcast([P, 2 * H, HD]), op=ALU.mult)\
                        .then_inc(s_kvr, 1)
                    dve.wait_ge(s_kvr, m + 1)
                    last = v_.tensor_reduce(kv[:, t, :].rearrange("p (a d) -> p a d", a=2),
                                            prod[:, :].rearrange("p (a h d) -> p a d h", a=2, h=H),
                                            axis=AX, op=ALU.add)
                    if t < TC - 1:
                        own(last)
                    else:
                        last.then_inc(s_kv, 1)
                        dve.wait_ge(s_kv, n + 1)
                    if t % 2 == 0:
                        b = t // 2
                        dve.wait_ge(s_q1, 2 * n + b + 1)
                        if n:
                            dve.wait_ge(s_q3, 2 * n)
                        v_.tensor_tensor(q_rest[:, b, :], ps_s[1][:, b, :], q_part[:, 0, b, :],
                                         op=ALU.subtract).then_inc(s_qr, 1)

            mxp_h = mxp[:, :, :].rearrange("p (h i) c -> p h i c", h=GH)

            def maxima(l, mc, mg0, it, uses):
                b0 = MB_ALL * l + before(max_banks, mc) + mg0 * max_banks(mc)
                for r, n in enumerate(uses):
                    if n == "row":
                        continue
                    dve.wait_ge(s_xmm, it * max_banks(mc) + (b0 + n + 1))
                    hh, i, _, w, _, piece = max_pieces(mc)[n][0]
                    heads = len(max_pieces(mc)[n])
                    v_.tensor_reduce(mxp_h[:, hh:hh + heads, i, piece],
                                     ps_x[r % RING][:, 0:heads * w].rearrange("p (h k) -> p h k", k=w),
                                     axis=AX, op=ALU.max).then_inc(s_xrd, 1)

            def join(l, mc, mg0, it):
                nv = NU * l + NG * mc + mg0
                b0 = MB_ALL * l + before(max_banks, mc) + mg0 * max_banks(mc)
                dve.wait_ge(s_xrd, it * max_banks(mc) + (b0 + max_banks(mc) + 2))
                v_.tensor_reduce(mxf[:, :], mxp[:, :, 0:mc + 1], axis=AX, op=ALU.max).then_inc(s_c1, 1)
                dve.wait_ge(s_c1, it + (nv + 1))
                dve.wait_ge(s_mt, it + (nv + 1))
                v_.tensor_copy(mx2[:, 0:GH * TC], mxf[:, :]).then_inc(s_c2, 1)
                dve.wait_ge(s_c2, it + (nv + 1))
                v_.tensor_tensor(mx2[:, GH * TC:], mxf[:, :], mx2[:, 0:GH * TC], op=ALU.subtract)\
                    .then_inc(s_mx, 1)
                dve.wait_ge(s_mx, it + (nv + 1))

            def unit(l, c, hf, it, last):
                un = NU * l + NG * c + 2 * hf
                nxt = ahead(l, c, hf)
                if nxt:
                    maxima(*nxt, it, ring(pair_steps(l, c, hf, last)))
                dve.wait_ge(s_ot, it + (un + 1))
                o = ps_o[:, :].rearrange("p (g e) -> p g e", e=VW)
                v_.reciprocal(rec[:, :], o[:, :, HD]).then_inc(s_rc, 1)
                dve.wait_ge(s_rc, it + (un + 1))
                dve.wait_ge(s_xa, it + (un + 1))
                v_.tensor_tensor(y_att[:, :, :], o[:, :, 0:HD],
                                 rec[:, :].unsqueeze(2).to_broadcast([P, GH * TC, HD]), op=ALU.mult)\
                    .then_inc(s_ya, 1)
                dve.wait_ge(s_ya, it + (un + 2))
                if nxt:
                    join(*nxt, it)

            def norms(l, c):
                k = branch_number(c)
                dve.wait_ge(s_xa, 1 + NG * (c + 1))
                if c:
                    dve.wait_ge(s_tp, branch_number(c - 1) + 2)
                layer_norm(k, bands(c), u1)
                layer_norm(k + 1, u1, u2)

            def turns(l, c):
                k = branch_number(c)
                dve.wait_ge(s_tp, k + 1)
                if c == 0:
                    dve.wait_ge(s_wld[2], 48)
                else:
                    dve.wait_ge(s_gp, 3 * c)
                v_.tensor_scalar(u2t[:, 1, :], ps_s[1][:, 1, :], gamma_c[:, 1:2], beta_c[:, 1:2],
                                 ALU.mult, ALU.add).then_inc(s_tb, 1)
                dve.wait_ge(s_tp, k + 2)
                if c:
                    dve.wait_ge(s_rp, 2 * c)
                v_.tensor_copy(g_xt[:, 1, :], ps_s[0][:, 1, :]).then_inc(s_tb, 1)

            def gates(l, c):
                dve.wait_ge(s_kp, c + 1)
                dve.wait_ge(s_gp, 3 * c + 2)
                v_.scalar_tensor_tensor(inp[:, :], ps_x[1][:, :], b_in_c[:, 1:2], alpha[:, :],
                                        ALU.add, ALU.mult).then_inc(s_in, 1)
                dve.wait_ge(s_in, c + 1)
                h0 = hst[:, (c - 1) % 2, QW - 1:QW] if c else 0.0
                if c:
                    dve.wait_ge(s_yr, c)
                v_.tensor_tensor_scan(hst[:, c % 2, :], keep[:, :], inp[:, :], h0, ALU.mult, ALU.add)\
                    .then_inc(s_h, 1)
                dve.wait_ge(s_h, c + 1)

            def branch(l, c):
                dve.wait_ge(s_xb, c + 1)
                for i in range(2):
                    dve.wait_ge(s_rp, 2 * c + i + 1)
                    xs = x_sb[:, TC * c + 2 * i:TC * c + 2 * i + 2, :].rearrange("p t d -> p (t d)")
                    v_.tensor_tensor(xs, ps_s[0][:, i, :], xs, op=ALU.add).then_inc(s_x2, 1)

            work = {"norm": norm, "turn": turn, "heads": heads, "norms": norms, "turns": turns,
                    "gates": gates, "branch": branch}
            for b, l, c, hf in pairs():
                for kind, ll, cc in SIDE[b]:
                    if kind in work:
                        work[kind](ll, cc)
                if b == 0:
                    for g0 in range(LAG):
                        maxima(0, 0, g0, 0, range(max_banks(0)))
                        join(0, 0, g0, 0)
                if ahead(l, c, hf):
                    with dve.Fori(0, 2) as it:
                        unit(l, c, hf, it, False)
                else:
                    unit(l, c, hf, 0, False)
                    unit(l, c, hf, 1, True)

        @block.tensor
        def _(pe):
            mm, tr = nc.tensor.matmul, nc.tensor.transpose
            pe.sem_inc(s_pv, 2)
            pe.sem_inc(s_mt, 1)

            pe.wait_ge(s_ident, 1)
            with pe.Fori(0, WARM_UP):
                for i in range(4):
                    mm(ps_s[1][:, 0, i * P:(i + 1) * P], ident[:, :], ident[:, :], start=True, stop=True)

            pe.wait_ge(s_wld[0], 32)
            for r in range(6):
                if r >= 2:
                    pe.wait_ge(s_wte, r - 1)
                for dc in range(DC):
                    last = tr(ps_s[r % 2][:, dc, 0:P], wqkv_n[:, r, dc * P:(dc + 1) * P], ident[:, :])
                last.then_inc(s_wt, 1)
            for dc in range(DC):
                last = tr(ps_x[0][:, dc * H:(dc + 1) * H], wg_n[:, dc * P:(dc + 1) * P], ident[0:H, 0:H])
            last.then_inc(s_wt, 1)
            pe.wait_ge(s_wte, 7)

            def transpose_rows(src, dst):
                for dc in range(DC):
                    for t in range(TC):
                        last = tr(dst[:, dc, t * P:(t + 1) * P], src[:, t, dc * P:(dc + 1) * P], ident[:, :])
                last.then_inc(s_tp, 1)

            def banks_left(k):
                if k:
                    pe.wait_ge(s_ta, k)
                    pe.wait_ge(s_tb, k)

            def turn(l, c):
                k = norm_number(l, c)
                pe.wait_ge(s_ln, k + 1)
                banks_left(k)
                if NCH * l + c:
                    pe.wait_ge(s_gd, NCH * l + c)
                transpose_rows(u, ps_s[0])

            def heads(l, c):
                n = NCH * l + c
                k = norm_number(l, c)
                pe.wait_ge(s_ta, k + 1)
                pe.wait_ge(s_tb, k + 1)
                for t in range(TC):
                    for dc in range(DC):
                        last = mm(gate_bank(t), ut[:, dc, t * P:(t + 1) * P], wg_t[:, dc, :],
                                  start=dc == 0, stop=dc == DC - 1)
                last.then_inc(s_gl, 1)
                for t in range(TC):
                    m = TC * n + t
                    if m >= RING:
                        pe.wait_ge(s_kvr, m - RING + 1)
                    for dc in range(DC):
                        last = mm(ps_x[m % RING][:, :], ut[:, dc, t * P:(t + 1) * P],
                                  wqkv_t[:, dc, D:3 * D], start=dc == 0, stop=dc == DC - 1)
                    last.then_inc(s_kvp, 1)
                    if t % 2 == 0:
                        b = t // 2
                        if n:
                            pe.wait_ge(s_qr, 2 * n)
                        if keys_before("heads", l, c):
                            pe.wait_ge(s_kt, keys_before("heads", l, c))
                        for dc in range(DC):
                            last = mm(ps_s[1][:, b, :], wqkv_t[:, dc, b * P:(b + 1) * P], ut[:, dc, :],
                                      start=dc == 0, stop=dc == DC - 1)
                        last.then_inc(s_qp, 1)

            def keys(l, c):
                n = NCH * l + c
                pe.wait_ge(s_krow, n + 1)
                pe.wait_ge(s_qr, 2 * heads_before(l, c))
                for t in range(TC):
                    last = tr(ps_k[:, t * P:(t + 1) * P], k_rows[:, t, :], ident_b[:, :])
                last.then_inc(s_ktp, 1)

            def max_bank(l, mc, mg0, it, n, bank):
                k_t = k_tl[:, l, :]
                for hh, i, key, w, col, piece in max_pieces(mc)[n]:
                    diag = piece == mc
                    q0 = it * UW + ((NG * mc + mg0) * UW + hh * QW + i * P)
                    last = mm(bank[:, col:col + w], q_t[0:KQ, bass.ds(q0, P)], k_t[0:KQ, key:key + w],
                              start=True, stop=not diag)
                    if diag:
                        last = mm(bank[:, col + w - P:col + w], ident_b[:, :], mask_qk[:, :],
                                  start=False, stop=True)
                last.then_inc(s_xmm, 1)

            def unit(l, c, hf, it, with_row):
                u_loc = NG * c + 2 * hf
                un = NU * l + u_loc
                s0 = SLOT_ALL * l + before(slots, c) + 2 * hf * slots(c)
                nxt = ahead(l, c, hf)
                if nxt:
                    ml, mc, mg0 = nxt
                    per = max_banks(mc)
                    b0 = MB_ALL * ml + before(max_banks, mc) + mg0 * per
                else:
                    per, b0 = 0, MB_ALL * 2
                steps = pair_steps(l, c, hf, not with_row)
                k_t, v_sb = k_tl[:, l, :], v_l[:, l, :, :]
                uses = ring(steps)
                pe.wait_ge(s_md, it * 16 + 16 * (un + 2))
                r = 0
                for kind, arg, _ in steps:
                    if kind == "qk":
                        j, hp = arg
                        kt, i = key_tile(c, j)
                        pe.wait_ge(s_exp, it * slots(c) + (s0 + 2 * j + hp + 1))
                        if j == 0 and hp == 1:
                            pe.wait_ge(s_qr, 2 * chunks_done("heads", l, c, hf))
                            pe.wait_ge(s_kt, chunks_done("keys", l, c, hf))
                        for hh in range(2):
                            q0 = it * UW + (u_loc * UW + (2 * hp + hh) * QW + P * i)
                            last = mm(ps_s[hp][:, hh, P * i:QW], k_t[0:KM, kt * P:(kt + 1) * P],
                                      q_t[0:KM, bass.ds(q0, QW - P * i)], start=True, stop=True)
                        last.then_inc(s_qk, 1)
                    elif kind == "pv":
                        j = arg
                        kt, i = key_tile(c, j)
                        if j < TC:
                            pe.wait_ge(s_msk, it * 2 * TC + (2 * TC * un + 2 * j + 2))
                        else:
                            pe.wait_ge(s_exp, it * slots(c) + (s0 + 2 * j + 4))
                        if j == 0:
                            pe.wait_ge(s_ya, it + (un + 1))
                        for hh in range(GH):
                            last = mm(ps_o[VW * hh:VW * hh + VW, P * i:QW], v_sb[:, kt, :],
                                      probs[:, j % 2, hh, P * i:QW], start=j == 0, stop=j == key_tiles(c) - 1)
                        last.then_inc(s_pv, 1)
                    else:
                        if r == 0:
                            pe.wait_ge(s_kvr, TC * chunks_done("heads", l, c, hf))
                        if r < RING:
                            pe.wait_ge(s_xrd, it * per + (b0 + 2))
                        elif uses[r - RING] == "row":
                            pe.wait_ge(s_mr, it + (un + 2))
                        else:
                            pe.wait_ge(s_xrd, it * per + (b0 + uses[r - RING] + 3))
                        if r == 0 and nxt:
                            pe.wait_ge(s_kt, NCH * ml + mc + 1)
                        if kind == "row":
                            pe.wait_ge(s_mx, it + (un + 2))
                            tr(as_rows(ps_x[r % RING]), mx2[:, :], ident_b[:, :]).then_inc(s_mt, 1)
                        else:
                            max_bank(ml, mc, mg0, it, arg, ps_x[r % RING])
                        r += 1
                pe.wait_ge(s_oe, it + (un + 2))
                if with_row:
                    pe.wait_ge(s_mr, it + (un + 2))
                for i in range(TC):
                    last = tr(ps_o[:, i * P:(i + 1) * P], o_sb[:, i * P:(i + 1) * P], ident[:, :])
                last.then_inc(s_ot, 1)

            def turns(l, c):
                k = branch_number(c)
                pe.wait_ge(s_ln, k + 2)
                banks_left(k)
                pe.wait_ge(s_kt, keys_before("turns", l, c))
                transpose_rows(u2, ps_s[1])
                transpose_rows(u1, ps_s[0])

            def gates(l, c):
                k = branch_number(c)
                pe.wait_ge(s_ta, k + 1)
                pe.wait_ge(s_tb, k + 1)
                if c == 0:
                    pe.wait_ge(s_wld[1], 48)
                for b, bank in enumerate(ps_x):
                    for dc in range(DC):
                        last = mm(bank[:, :], w_in_sb[:, dc, b * S:(b + 1) * S], u2t[:, dc, :],
                                  start=dc == 0, stop=dc == DC - 1)
                    last.then_inc(s_gp, 1)

            def gates_read(c):
                pe.wait_ge(s_al, c + 1)
                pe.wait_ge(s_in, c + 1)
                pe.wait_ge(s_tc, c + 1)

            def branch(l, c):
                pe.wait_ge(s_yr, c + 1)
                pe.wait_ge(s_ta, branch_number(c) + 2)
                pe.wait_ge(s_tb, branch_number(c) + 2)
                pe.wait_ge(s_gd, NCH + c)
                for t in range(TC):
                    o = ps_s[0][:, t // 2, (t % 2) * D:(t % 2 + 1) * D]
                    mm(o, y_rec[:, t * P:(t + 1) * P], w_out_sb[:, :], start=True, stop=False)
                    mm(o, g_xt[:, 0, t * P:(t + 1) * P], w_skip_sb[:, 0, :], start=False, stop=False)
                    last = mm(o, g_xt[:, 1, t * P:(t + 1) * P], w_skip_sb[:, 1, :], start=False, stop=True)
                    if t % 2:
                        last.then_inc(s_rp, 1)

            def leave(kind, l, c):
                n = NCH * l + c
                if kind in ("turn", "turns"):
                    k = norm_number(l, c) if kind == "turn" else branch_number(c) + 1
                    pe.wait_ge(s_ta, k + 1)
                    pe.wait_ge(s_tb, k + 1)
                elif kind == "heads":
                    pe.wait_ge(s_gd, n + 1)
                elif kind == "gates":
                    gates_read(c)
                elif kind == "branch":
                    pe.wait_ge(s_x2, 2 * c + 2)

            work = {"turn": turn, "heads": heads, "keys": keys, "turns": turns, "gates": gates,
                    "branch": branch}
            for b, l, c, hf in pairs():
                if any(kind in work for kind, _, _ in SIDE[b]) and b:
                    un = NU * l + NG * c + 2 * hf
                    s0 = SLOT_ALL * l + before(slots, c) + 2 * hf * slots(c)
                    pe.wait_ge(s_exp, s0 + 2)
                    nxt = ahead(l, c, hf)
                    if nxt and any(kind in ("heads", "gates") for kind, _, _ in SIDE[b]):
                        ml, mc, mg0 = nxt
                        pe.wait_ge(s_xrd, MB_ALL * ml + before(max_banks, mc) + mg0 * max_banks(mc) + 2)
                done = []
                for kind, ll, cc in SIDE[b]:
                    if kind in work:
                        if kind == "heads":
                            for k2, _, c2 in done:
                                if k2 == "gates":
                                    gates_read(c2)
                        work[kind](ll, cc)
                        done.append((kind, ll, cc))
                for kind, ll, cc in done:
                    leave(kind, ll, cc)
                nxt = ahead(l, c, hf)
                if b == 0:
                    for r in range(len(Q_PART)):
                        pe.wait_ge(s_qt[r], 16 * DC)
                    pe.wait_ge(s_kt, 1)
                    pe.wait_ge(s_kvr, TC * chunks_done("heads", 0, 0, 0))
                    for g0 in range(LAG):
                        for n in range(max_banks(0)):
                            pe.wait_ge(s_xrd, g0 * max_banks(0) + 2 + max(0, n + 1 - RING))
                            max_bank(0, 0, g0, 0, n, ps_x[n % RING])
                            if g0 and n == RING:
                                pe.wait_ge(s_mx, 1)
                                tr(as_rows(ps_o), mx2[:, :], ident_b[:, :]).then_inc(s_mt, 1)
                    pe.wait_ge(s_mr, 1)
                    pe.wait_ge(s_xrd, LAG * max_banks(0) + 2)
                if nxt and nxt[2] == 0:
                    n = NCH * nxt[0] + nxt[1]
                    for r in range(len(Q_PART)):
                        pe.wait_ge(s_qt[r], 16 * DC * (n + 1))
                if nxt:
                    with pe.Fori(0, 2) as it:
                        unit(l, c, hf, it, True)
                else:
                    unit(l, c, hf, 0, True)
                    unit(l, c, hf, 1, False)


_INS = ['L0_attn_x', 'L0_attn_gamma', 'L0_attn_beta', 'L0_attn_W_in', 'L0_attn_b_in', 'L0_attn_W_out',
        'L0_attn_b_out', 'L0_attn_W_skip', 'L0_attn_b_skip', 'L0_ffn_W_gate', 'L0_ffn_W_qkv']
_OUTS = [((1, T, D), 'float32')]


def kernel(**inputs):
    import numpy as _np
    import concourse.bacc as _bacc
    from concourse import mybir as _mybir
    from concourse.bass_utils import run_bass_kernel_spmd as _run

    nc = _bacc.Bacc("TRN2", target_bir_lowering=False, num_devices=1)
    arrays, args = {}, []
    for name in _INS:
        a = _np.ascontiguousarray(inputs[name])
        arrays[f"in_{name}_dram"] = a
        args.append(nc.dram_tensor(f"in_{name}_dram", a.shape, _mybir.dt.from_np(a.dtype), kind="ExternalInput").ap())
    for i, (shape, dtype) in enumerate(_OUTS):
        dt = _mybir.dt.from_np(_np.dtype(dtype))
        args.append(nc.dram_tensor(f"out_{i}_dram", shape, dt, kind="ExternalOutput").ap())
    macaron_block(nc, *args)
    r = _run(nc, [arrays], core_ids=[0])
    got = tuple(r.results[0][f"out_{i}_dram"] for i in range(len(_OUTS)))
    return got[0]
```
